# Optimizing a Trainium2 kernel written in Bass

```python
import numpy as np
import jax
import jax.numpy as jnp

def _softmax(x, axis=-1):
    return jax.nn.softmax(x, axis=axis)

def _gelu(x):
    return jax.nn.gelu(x, approximate=True)

def _silu(x):
    return jax.nn.silu(x)

def _sigmoid(x):
    return jax.nn.sigmoid(x)

def _layernorm(x, axis=-1, eps=1e-05):
    m = jnp.mean(x, axis=axis, keepdims=True)
    v = jnp.var(x, axis=axis, keepdims=True)
    return (x - m) / jnp.sqrt(v + eps)

def _scatter_add(tgt, idx, src, axis=0):
    return tgt.at[idx].add(src)

def _segment_sum(src, seg, n):
    return jax.ops.segment_sum(src, seg, n)
kernel_name = 'mk_gnn_preln_d4_gnn_r8_3bf275'

def setup_inputs(seed: int=0):
    np.random.seed(seed)
    _w = jnp.asarray

    def _rec_inputs():
        import jax
        import jax.numpy as jnp
        _gk = jax.random.key(seed)
        x = -0.0005121 + 1.001 * jax.random.normal(jax.random.fold_in(_gk, 1), (6250, 64), jnp.float32)
        src = jax.random.randint(jax.random.fold_in(_gk, 2), (200000,), 0, 6250, jnp.int32)
        dst = jax.random.randint(jax.random.fold_in(_gk, 3), (200000,), 0, 6250, jnp.int32)
        _o = jnp.argsort(dst, stable=True)
        src = src[_o]
        dst = dst[_o]
        edge_type_8 = jax.random.randint(jax.random.fold_in(_gk, 13), (200000,), 0, 8, jnp.int32)
        edge_weight = jax.random.uniform(jax.random.fold_in(_gk, 14), (200000,), jnp.float32, 0.0, 1)
        return (x, src, dst, edge_type_8, edge_weight)
    x, src, dst, edge_type_8, edge_weight = _rec_inputs()

    def _L0_gnn_setup():
        import jax, jax.numpy as jnp
        import numpy as np
        N_NODES = 6250
        key = jax.random.key(seed)
        k = jax.random.split(key, 7)
        N, E, D = (N_NODES, 100000, 64)
        x = jax.random.normal(k[0], (N, D), dtype=jnp.float32)
        edge_src = jax.random.randint(k[1], (E,), 0, N, dtype=jnp.int32)
        edge_dst = jax.random.randint(k[2], (E,), 0, N, dtype=jnp.int32)
        s1 = 1.0 / np.sqrt(D)
        w1 = jax.random.uniform(k[3], (D, D), jnp.float32, -s1, s1)
        b1 = jax.random.uniform(k[4], (D,), jnp.float32, -s1, s1)
        w2 = jax.random.uniform(k[5], (D, D), jnp.float32, -s1, s1)
        b2 = jax.random.uniform(k[6], (D,), jnp.float32, -s1, s1)
        return {'x': x, 'edge_src': edge_src, 'edge_dst': edge_dst, 'w1': w1, 'b1': b1, 'w2': w2, 'b2': b2}
    _L0_gnn_all = _L0_gnn_setup()
    _L0_gnn_in = {k: v for k, v in _L0_gnn_all.items() if k in ('w1', 'b1', 'w2', 'b2')}
    del _L0_gnn_all

    def _L1_gnn_setup():
        import jax, jax.numpy as jnp
        import numpy as np
        N_NODES = 12500
        N_EDGES = 200000
        IN_CH = 64
        OUT_CH = 64
        key = jax.random.key(seed)
        k1, k2, k3, k4 = jax.random.split(key, 4)
        x = jax.random.normal(k1, (N_NODES, IN_CH), dtype=jnp.float32)
        edge_index = jax.random.randint(k2, (2, N_EDGES), 0, N_NODES, dtype=jnp.int64)
        W1 = jax.random.normal(k3, (2 * IN_CH, OUT_CH), dtype=jnp.float32) * (1.0 / np.sqrt(2 * IN_CH))
        b1 = jnp.zeros((OUT_CH,), dtype=jnp.float32)
        W2 = jax.random.normal(k4, (OUT_CH, OUT_CH), dtype=jnp.float32) * (1.0 / np.sqrt(OUT_CH))
        b2 = jnp.zeros((OUT_CH,), dtype=jnp.float32)
        return {'x': x, 'edge_index': edge_index, 'W1': W1, 'b1': b1, 'W2': W2, 'b2': b2}
    _L1_gnn_all = _L1_gnn_setup()
    _L1_gnn_in = {k: v for k, v in _L1_gnn_all.items() if k in ('W1', 'b1', 'W2', 'b2')}
    del _L1_gnn_all

    def _L2_gnn_setup():
        import jax, jax.numpy as jnp
        import numpy as np
        N_NODES = 6250
        N_EDGES = 100000
        D_IN = 64
        D_OUT = 64
        key = jax.random.key(seed)
        ks = jax.random.split(key, 8)
        feat = jax.random.normal(ks[0], (N_NODES, D_IN), dtype=jnp.float32)
        weight = jax.random.uniform(ks[1], (N_EDGES,), dtype=jnp.float32)
        W_self = jax.random.normal(ks[2], (D_OUT, D_IN), dtype=jnp.float32) * 0.1
        b_self = jax.random.normal(ks[3], (D_OUT,), dtype=jnp.float32) * 0.1
        W_neigh = jax.random.normal(ks[4], (D_OUT, D_IN), dtype=jnp.float32) * 0.1
        b_neigh = jax.random.normal(ks[5], (D_OUT,), dtype=jnp.float32) * 0.1
        src = jax.random.randint(ks[6], (N_EDGES,), 0, N_NODES, dtype=jnp.int64)
        dst = jax.random.randint(ks[7], (N_EDGES,), 0, N_NODES, dtype=jnp.int64)
        return {'feat': feat, 'weight': weight, 'W_self': W_self, 'b_self': b_self, 'W_neigh': W_neigh, 'b_neigh': b_neigh, 'src': src, 'dst': dst}
    _L2_gnn_all = _L2_gnn_setup()
    _L2_gnn_in = {k: v for k, v in _L2_gnn_all.items() if k in ('W_self', 'b_self', 'W_neigh', 'b_neigh')}
    del _L2_gnn_all

    def _L3_gnn_setup():
        import jax, jax.numpy as jnp
        import numpy as np
        N_NODES = 6250
        N_EDGES = 100000
        D_IN, D_HID, D_OUT = (64, 64, 64)
        N_REL, N_BASES = (8, 4)

        def _per_edge_inv_deg(dst, edge_type, n_nodes, n_rel):
            deg = jnp.zeros((n_rel, n_nodes), jnp.float32).at[edge_type, dst].add(1.0)
            return 1.0 / jnp.maximum(deg[edge_type, dst], 1.0)

        def _rgcn_conv(x, src, dst, edge_type, inv_deg, basis, comp, root, bias):
            n_nodes = x.shape[0]
            xs = x[src]
            c = comp[edge_type]
            m = c[:, 0:1] * (xs @ basis[0])
            for b in range(1, basis.shape[0]):
                m = m + c[:, b:b + 1] * (xs @ basis[b])
            agg = jax.ops.segment_sum(m * inv_deg[:, None], dst, num_segments=n_nodes)
            return agg + x @ root + bias
        key = jax.random.key(seed)
        ks = jax.random.split(key, 12)
        x = jax.random.normal(ks[0], (N_NODES, D_IN), dtype=jnp.float32)
        src = jax.random.randint(ks[1], (N_EDGES,), 0, N_NODES)
        dst = jax.random.randint(ks[2], (N_EDGES,), 0, N_NODES)
        edge_index = jnp.stack([src, dst]).astype(jnp.int64)
        edge_type = jax.random.randint(ks[3], (N_EDGES,), 0, N_REL).astype(jnp.int64)
        s = 0.1
        return {'x': x, 'edge_index': edge_index, 'edge_type': edge_type, 'basis1': jax.random.normal(ks[4], (N_BASES, D_IN, D_HID), jnp.float32) * s, 'comp1': jax.random.normal(ks[5], (N_REL, N_BASES), jnp.float32) * s, 'root1': jax.random.normal(ks[6], (D_IN, D_HID), jnp.float32) * s, 'bias1': jnp.zeros((D_HID,), jnp.float32), 'basis2': jax.random.normal(ks[7], (N_BASES, D_HID, D_OUT), jnp.float32) * s, 'comp2': jax.random.normal(ks[8], (N_REL, N_BASES), jnp.float32) * s, 'root2': jax.random.normal(ks[9], (D_HID, D_OUT), jnp.float32) * s, 'bias2': jnp.zeros((D_OUT,), jnp.float32)}
    _L3_gnn_all = _L3_gnn_setup()
    _L3_gnn_in = {k: v for k, v in _L3_gnn_all.items() if k in ('basis1', 'comp1', 'root1', 'bias1', 'basis2', 'comp2', 'root2', 'bias2')}
    del _L3_gnn_all
    return {'x': x, 'src': src, 'dst': dst, 'edge_type_8': edge_type_8, 'edge_weight': edge_weight, 'L0_gnn_w1': _L0_gnn_in['w1'], 'L0_gnn_b1': _L0_gnn_in['b1'], 'L0_gnn_w2': _L0_gnn_in['w2'], 'L0_gnn_b2': _L0_gnn_in['b2'], 'L1_gnn_W1': _L1_gnn_in['W1'], 'L1_gnn_b1': _L1_gnn_in['b1'], 'L1_gnn_W2': _L1_gnn_in['W2'], 'L1_gnn_b2': _L1_gnn_in['b2'], 'L2_gnn_W_self': _L2_gnn_in['W_self'], 'L2_gnn_b_self': _L2_gnn_in['b_self'], 'L2_gnn_W_neigh': _L2_gnn_in['W_neigh'], 'L2_gnn_b_neigh': _L2_gnn_in['b_neigh'], 'L3_gnn_basis1': _L3_gnn_in['basis1'], 'L3_gnn_comp1': _L3_gnn_in['comp1'], 'L3_gnn_root1': _L3_gnn_in['root1'], 'L3_gnn_bias1': _L3_gnn_in['bias1'], 'L3_gnn_basis2': _L3_gnn_in['basis2'], 'L3_gnn_comp2': _L3_gnn_in['comp2'], 'L3_gnn_root2': _L3_gnn_in['root2'], 'L3_gnn_bias2': _L3_gnn_in['bias2']}

def reference(x, src, dst, edge_type_8, edge_weight, L0_gnn_w1, L0_gnn_b1, L0_gnn_w2, L0_gnn_b2, L1_gnn_W1, L1_gnn_b1, L1_gnn_W2, L1_gnn_b2, L2_gnn_W_self, L2_gnn_b_self, L2_gnn_W_neigh, L2_gnn_b_neigh, L3_gnn_basis1, L3_gnn_comp1, L3_gnn_root1, L3_gnn_bias1, L3_gnn_basis2, L3_gnn_comp2, L3_gnn_root2, L3_gnn_bias2):
    import jax
    import jax.numpy as jnp

    def _L0_gnn_ref(x, edge_src, edge_dst, w1, b1, w2, b2):
        import jax, jax.numpy as jnp
        import numpy as np
        N_NODES = 6250
        N = N_NODES
        ones = jnp.ones(edge_src.shape[0], dtype=jnp.float32)
        out_deg = jax.ops.segment_sum(ones, edge_src, num_segments=N)
        in_deg = jax.ops.segment_sum(ones, edge_dst, num_segments=N)
        prod = out_deg[edge_src] * in_deg[edge_dst]
        prod = jnp.where(prod == 0, 1.0, prod)
        norm = jax.lax.rsqrt(prod)
        msg = x[edge_src] * norm[:, None]
        agg = jax.ops.segment_sum(msg, edge_dst, num_segments=N)
        h = jnp.einsum('nd,dh->nh', agg, w1) + b1
        h = jax.nn.gelu(h, approximate=False)
        out = jnp.einsum('nh,hd->nd', h, w2) + b2
        return out

    def _L1_gnn_ref(x, edge_index, W1, b1, W2, b2):
        import jax, jax.numpy as jnp
        import numpy as np
        N_NODES = 12500
        N_EDGES = 200000
        IN_CH = 64
        OUT_CH = 64
        src = edge_index[0]
        dst = edge_index[1]
        xi = x[dst]
        xj = x[src]
        h = jnp.concatenate([xi, xj - xi], axis=-1)
        h = jax.nn.relu(h @ W1 + b1)
        h = jax.nn.relu(h @ W2 + b2)
        out = jax.ops.segment_max(h, dst, num_segments=x.shape[0])
        return jnp.where(jnp.isfinite(out), out, jnp.zeros_like(out))

    def _L2_gnn_ref(feat, weight, W_self, b_self, W_neigh, b_neigh, src, dst):
        import jax, jax.numpy as jnp
        import numpy as np
        N_NODES = 6250
        N_EDGES = 100000
        D_IN = 64
        D_OUT = 64
        n = feat.shape[0]
        msg = feat[src] * weight[:, None]
        neigh_sum = jax.ops.segment_sum(msg, dst, num_segments=n)
        deg = jax.ops.segment_sum(jnp.ones_like(weight), dst, num_segments=n)
        h_neigh = neigh_sum / jnp.maximum(deg, 1.0)[:, None]
        rst = feat @ W_self.T + b_self + (h_neigh @ W_neigh.T + b_neigh)
        return rst

    def _L3_gnn_ref(x, edge_index, edge_type, basis1, comp1, root1, bias1, basis2, comp2, root2, bias2):
        import jax, jax.numpy as jnp
        import numpy as np
        N_NODES = 6250
        N_EDGES = 100000
        D_IN, D_HID, D_OUT = (64, 64, 64)
        N_REL, N_BASES = (8, 4)

        def _per_edge_inv_deg(dst, edge_type, n_nodes, n_rel):
            deg = jnp.zeros((n_rel, n_nodes), jnp.float32).at[edge_type, dst].add(1.0)
            return 1.0 / jnp.maximum(deg[edge_type, dst], 1.0)

        def _rgcn_conv(x, src, dst, edge_type, inv_deg, basis, comp, root, bias):
            n_nodes = x.shape[0]
            xs = x[src]
            c = comp[edge_type]
            m = c[:, 0:1] * (xs @ basis[0])
            for b in range(1, basis.shape[0]):
                m = m + c[:, b:b + 1] * (xs @ basis[b])
            agg = jax.ops.segment_sum(m * inv_deg[:, None], dst, num_segments=n_nodes)
            return agg + x @ root + bias
        src, dst = (edge_index[0], edge_index[1])
        inv_deg = _per_edge_inv_deg(dst, edge_type, x.shape[0], comp1.shape[0])
        h = _rgcn_conv(x, src, dst, edge_type, inv_deg, basis1, comp1, root1, bias1)
        h = jax.nn.relu(h)
        return _rgcn_conv(h, src, dst, edge_type, inv_deg, basis2, comp2, root2, bias2)
    edge_index = jnp.stack([src, dst])
    h = jnp.maximum(_layernorm(x, axis=-1), 0.0)
    x = x + _L0_gnn_ref(h, src, dst, L0_gnn_w1, L0_gnn_b1, L0_gnn_w2, L0_gnn_b2)
    h = jnp.maximum(_layernorm(x, axis=-1), 0.0)
    x = x + _L1_gnn_ref(h, edge_index, L1_gnn_W1, L1_gnn_b1, L1_gnn_W2, L1_gnn_b2)
    h = jnp.maximum(_layernorm(x, axis=-1), 0.0)
    x = x + _L2_gnn_ref(h, edge_weight, L2_gnn_W_self, L2_gnn_b_self, L2_gnn_W_neigh, L2_gnn_b_neigh, src, dst)
    h = jnp.maximum(_layernorm(x, axis=-1), 0.0)
    x = x + _L3_gnn_ref(h, edge_index, edge_type_8, L3_gnn_basis1, L3_gnn_comp1, L3_gnn_root1, L3_gnn_bias1, L3_gnn_basis2, L3_gnn_comp2, L3_gnn_root2, L3_gnn_bias2)
    return x

_drawn_inputs = setup_inputs


def setup_inputs(seed=0):
    import zlib

    import numpy as np

    out = dict(_drawn_inputs(seed))
    spreads = {'L1_gnn_b1': (0.0, 0.1),
     'L1_gnn_b2': (0.0, 0.1),
     'L3_gnn_bias1': (0.0, 0.1),
     'L3_gnn_bias2': (0.0, 0.1)}
    factors = {'L0_gnn_b1': 2.982}
    for name, (base, spread) in spreads.items():
        noise = np.random.default_rng([zlib.crc32(name.encode()), seed]).standard_normal(out[name].shape)
        drawn = base * np.exp(spread * noise) if base else spread * noise
        out[name] = jnp.asarray(drawn.astype(out[name].dtype))
    for name, factor in factors.items():
        out[name] = (out[name] * factor).astype(out[name].dtype)
    return out
```

```python
import concourse.bass as bass
from concourse import mybir
from contextlib import ExitStack

N = 6250
E = 200000
D = 64
T = 8
NB = 4
P = 128
J = 50
NPAD = P * J
G = 4
SC = P * G
K = 4
NI = -(-E // (SC * K))
NS = NI * K
EP = NS * SC
NCH = NS * G
AW = D + T
JG = 10
NG = J // JG
HB = 8
NHB = NCH // HB
PEEL = 2
EPS = 1e-5
ROUND = 1.5 * 2.0 ** 23


def gnn_kernel(nc, x, src, dst, typ, wgt, dst_row, prev_row, typ_row,
               gcn_w1, gcn_b1, gcn_w2, gcn_b2,
               edge_w1, edge_b1, edge_w2, edge_b2,
               self_wT, self_b, neigh_wT, neigh_b,
               basis1, comp1, root1, bias1, basis2, comp2, root2, bias2, out):
    f32, f16, bf16, i32 = mybir.dt.float32, mybir.dt.float16, mybir.dt.bfloat16, mybir.dt.int32
    ALU = mybir.AluOpType
    ACT = mybir.ActivationFunctionType
    AX = mybir.AxisListType

    tab = nc.dram_tensor("node_table", [NPAD, D], f32).ap()
    ytab = nc.dram_tensor("typed_table", [NPAD * T, D], f32).ap()
    spread = nc.dram_tensor("spread_table", [EP + NPAD, AW], f32).ap()
    scans = nc.dram_tensor("scan_rows", [EP, D], f32).ap()
    keep_d = nc.dram_tensor("keep_row", [EP + K * SC], bf16).ap()
    typ_d = nc.dram_tensor("type_row", [EP + K * SC], bf16).ap()

    with ExitStack() as ctx:
        def sb(name, shape, dt=f32):
            return ctx.enter_context(nc.sbuf_tensor(name, shape, dt))

        def sem(name):
            return ctx.enter_context(nc.semaphore(name))

        src_i = sb("src_i", [P, NCH + K * G], i32)
        srct_i = sb("srct_i", [P, NCH + K * G], i32)
        wgt_s = sb("wgt_s", [P, NCH])
        inv_s = sb("inv_s", [P, NCH])
        hi_s = sb("hi_s", [P, NCH], f16)
        lo_s = sb("lo_s", [P, NCH], f16)

        xs = sb("xs", [P, J, D])
        hs = sb("hs", [P, J, D])
        ws = sb("ws", [P, J, D])
        es = sb("es", [P, J, D])
        rs = sb("rs", [P, J, D])
        ax = sb("ax", [P, J, AW])
        cnt = sb("cnt", [P, J, T])
        odeg = sb("odeg", [P, J])
        deg = sb("deg", [P, J])
        dmask = sb("dmask", [P, J])
        gcnf = sb("gcnf", [P, J])
        meanf = sb("meanf", [P, J])
        csum = sb("csum", [P, J])
        pre = sb("pre", [P, 1])
        st = [sb(f"st{n}", [P, J]) for n in range(3)]
        end_i = sb("end_i", [P, J], i32)
        start_i = sb("start_i", [P, J], i32)

        def part(t, n, w=NCH):
            return t[:, :, :].rearrange("p j d -> p (j d)")[:, n * w:n * w + w]

        dst_e, fa = part(es, 0), part(es, 1)
        fb, typ_e = part(rs, 0), part(rs, 1)
        row_d, row_p = part(ax, 0), part(ax, 1)

        ident = sb("ident", [P, P])
        lower = sb("lower", [P, P])
        iota_hi = sb("iota_hi", [P, P, HB], f16)
        iota_lo = sb("iota_lo", [P, J, HB], f16)
        iota_lt = sb("iota_lt", [P, J * T, G], f16)
        nid = sb("nid", [P, J])
        typc = sb("typc", [P, 1])
        ones = sb("ones", [P, J])
        bd = {n: sb(f"bd_{n}", [P, P]) for n in ("g1", "g2", "ea", "eb", "sf", "ng", "r1", "r2")}
        bias = {n: sb(f"bias_{n}", [P, D]) for n in ("g1", "g2", "ea", "sf", "ng", "r1", "r2")}
        ew2 = sb("ew2", [D, D])
        eb2 = sb("eb2", [D, 1])
        wz = [sb(f"wz{n}", [P, 2, T * D]) for n in range(2)]
        zrow = 28 * AW
        zero = sb("zero", [P, zrow])
        bas = [sb(f"bas{n}", [P, NB, D]) for n in range(2)]
        com = [sb(f"com{n}", [P, T, NB]) for n in range(2)]

        idx = sb("idx", [P, K, G], i32)
        gat = sb("gat", [P, K, G, D])
        keep = sb("keep", [AW, K, SC], bf16)
        typb = sb("typb", [AW, K, SC], bf16)
        dmp = sb("dmp", [P, K, G, D])
        scn = sb("scn", [D, 2, SC])
        oh = sb("oh", [P, 2, P, HB], f16)
        ol = sb("ol", [P, 2, J, HB], f16)
        olt = sb("olt", [P, 2, J * T, G], f16)
        tsl = sb("tsl", [P, 2, JG * D])

        cuts = [K * G * AW, 2 * SC, 2 * SC, 2 * SC, 2 * SC]
        shared = sb("shared", [P, max(sum(cuts), 2 * 5 * T * D)])
        at = [sum(cuts[:n]) for n in range(len(cuts))]
        axe = shared[:, 0:cuts[0]].rearrange("p (k g d) -> p k g d", k=K, g=G)
        fil, tpr, hsm, zed = (shared[:, a:a + c].rearrange("p (b n) -> p b n", b=2)
                              for a, c in zip(at[1:], cuts[1:]))
        ysl = shared[:, 0:2 * 5 * T * D].rearrange("p (b j n) -> p b j n", b=2, j=5)
        wprod = shared[:, 0:T * NB * D].rearrange("p (t b o) -> p t b o", t=T, b=NB)
        row_t = shared[:, 0:NCH]
        keep_r = shared[:, NCH:NCH + NCH // 2].bitcast(bf16)
        typ_r = shared[:, 2 * NCH:2 * NCH + NCH // 2].bitcast(bf16)

        ps = ctx.enter_context(nc.psum_tensor("ps", [P, 8 * 512], f32))

        def bank(n, w=512):
            return ps[:, 512 * n:512 * n + w]

        def wide(n):
            return ps[:, 1024 * n:1024 * n + JG * D]

        s_edge = sem("edges_loaded")
        s_x = sem("x_loaded")
        s_row = sem("rows_loaded")
        s_w = sem("weights_loaded")
        s_const = sem("constants_made")
        s_zs = sem("zero_tiles_made")
        s_zero = sem("spread_table_zeroed")
        s_rowd = sem("flag_rows_written")
        s_flag = sem("flag_rows_made")
        s_v = sem("vector_chain")
        s_oh = sem("source_onehots_made")
        s_hist = sem("source_batches_counted")
        s_histr = sem("source_batches_added")
        s_coh = sem("target_onehots_made")
        s_cc = sem("target_superchunks_counted")
        s_ccr = sem("target_superchunks_added")
        s_tabrdy = sem("table_values_ready")
        s_tab = sem("table_written")
        s_tot = sem("partition_totals_ready")
        s_pre = sem("partition_prefix_summed")
        s_endi = sem("end_index_ready")
        s_sprd = sem("spread_rows_ready")
        s_scat = sem("spread_rows_scattered")
        s_ends = sem("end_rows_gathered")
        s_idx = sem("index_slots_filled")
        s_gat = [sem(f"rows_gathered{k}") for k in range(K)]
        s_scl = sem("rows_scaled")
        s_turn = sem("rows_transposed")
        s_scan = sem("superchunks_scanned")
        s_back = sem("scans_transposed_back")
        s_evac = sem("scan_rows_evacuated")
        s_dump = [sem(f"scan_rows_dumped{k}") for k in range(K)]
        s_keep = [sem(f"keep_loaded{k}") for k in range(K)]
        s_axe = [sem(f"spread_rows_loaded{k}") for k in range(K)]
        s_fil = sem("target_rows_filled")
        s_hsum = sem("edge_hidden_summed")
        s_tpr = sem("type_products_made")
        s_relu = sem("edge_hidden_rectified")
        s_mlp = sem("edge_mlp_multiplied")
        s_zed = sem("edge_mlp_rectified")
        s_wsum = sem("inverse_counts_summed")
        s_wev = sem("inverse_counts_kept")
        s_lin = sem("node_features_ready")
        s_lt = sem("node_groups_transposed")
        s_lc = sem("node_transposes_copied")
        s_lm = sem("node_groups_multiplied")
        s_le = sem("node_products_read")
        s_ym = sem("typed_columns_multiplied")
        s_yv = sem("typed_columns_read_by_vector")
        s_ya = sem("typed_columns_read_by_scalar")
        s_yd = [sem(f"typed_rows_written{k}") for k in range(2)]
        s_sq = sem("sqrt_input_ready")
        s_rt = sem("sqrt_done")
        s_gi = sem("gelu_input_ready")
        s_go = sem("gelu_done")
        s_go_pool = sem("gathers_begun")
        s_go_pe = sem("products_begun")
        s_fin = sem("result_ready")
        s_out = sem("result_written")

        MLP = 1
        NPASS = 5
        idx_tab = [src_i, src_i, src_i, srct_i, srct_i]
        wgt_tab = [None, None, wgt_s, inv_s, inv_s]
        IDXF = NS + K
        KEEPF = NI + 1
        LIN = ["g1", "g2", "ea", "eb", "sf", "ng", "y0", "r1", "y1", "r2"]
        HY = J // 2

        def plain_before(n):
            return sum(not m.startswith("y") for m in LIN[:n])

        def since(eng, semaphore, value):
            if not isinstance(value, int) or value > 0:
                eng.wait_ge(semaphore, value)

        def steps(eng, count, per, body, lag=0):
            for i in range(PEEL):
                for k in range(per):
                    body(per * i + k, i, k, lambda n, s=per * i + k: s >= n)
            with eng.Fori(PEEL, count) as i:
                for k in range(per):
                    body(i * per + k, i, k, lambda n: True)
            for k in range(lag):
                body(per * count + k, count, k, lambda n, k=k: n > k)

        def lagged(i, k, lag):
            return (i if k >= lag else i - 1), (k - lag) % K

        zero_rows = EP + NPAD
        zero_per = zrow // AW * P
        zero_parts = -(-zero_rows // zero_per)
        n_w = 2 * len(bd) + len(bias) + 2 + 6 + 1

        block = ctx.enter_context(nc.Block())

        @block.sync
        def _(sp):
            sp.dma_start(src_i[:, 0:NCH], src).then_inc(s_edge, 16)
            sp.dma_start(xs[:, :, :], x.rearrange("(p j) d -> p j d", j=J)).then_inc(s_x, 16)
            sp.dma_start(row_d.bitcast(i32), dst_row).then_inc(s_row, 16)
            sp.dma_start(row_p.bitcast(i32), prev_row).then_inc(s_row, 16)
            sp.dma_start(row_t.bitcast(i32), typ_row).then_inc(s_row, 16)
            sp.dma_start(dst_e.bitcast(i32), dst).then_inc(s_row, 16)
            sp.dma_start(typ_e.bitcast(i32), typ).then_inc(s_row, 16)
            sp.wait_ge(s_flag, 1)
            pad = K * SC // P
            for row_dram, row in ((keep_d, keep_r), (typ_d, typ_r)):
                sp.dma_start(row_dram[0:EP].rearrange("(p m) -> p m", p=P), row).then_inc(s_rowd, 16)
                sp.dma_start(row_dram[EP:EP + K * SC].rearrange("(p m) -> p m", p=P), row[:, 0:pad]
                             ).then_inc(s_rowd, 16)
            sp.wait_ge(s_zs, 1)
            for n, (w, b) in {"g1": (gcn_w1, gcn_b1), "g2": (gcn_w2, gcn_b2),
                              "ea": (edge_w1[0:D, :], edge_b1), "eb": (edge_w1[D:2 * D, :], None),
                              "sf": (self_wT, self_b), "ng": (neigh_wT, neigh_b),
                              "r1": (root1, bias1), "r2": (root2, bias2)}.items():
                sp.dma_start(bd[n][0:D, 0:D], w).then_inc(s_w, 16)
                sp.dma_start(bd[n][D:P, D:P], w).then_inc(s_w, 16)
                if b is not None:
                    sp.dma_start(bias[n][:, :], b[None, :].to_broadcast([P, D])).then_inc(s_w, 16)
            sp.dma_start(ew2[:, :], edge_w2).then_inc(s_w, 16)
            sp.dma_start(eb2[:, :], edge_b2[:, None]).then_inc(s_w, 16)
            for n, (ba, co) in enumerate(((basis1, comp1), (basis2, comp2))):
                for h in range(2):
                    sp.dma_start(bas[n][D * h:D * h + D, :, :], ba.rearrange("b i o -> i b o")).then_inc(s_w, 16)
                sp.dma_start(com[n][:, :, :], co[None, :, :].to_broadcast([P, T, NB])).then_inc(s_w, 16)
            sp.dma_start(wgt_s[:, :], wgt).then_inc(s_w, 16)
            sp.wait_ge(s_rowd, 64)

            def table(q, rows):
                sp.wait_ge(s_tabrdy, q + 1)
                sp.dma_start(tab.rearrange("(p j) d -> p j d", j=J), rows[:, :, :]).then_inc(s_tab, 16)

            def typed_table(m):
                rows = ytab.rearrange("(p j t) d -> p j (t d)", j=J, t=T)
                for y in range(J // 5):
                    c = 5 * y + 5
                    sp.wait_ge(s_yv, m * HY + (c + 1) // 2)
                    sp.wait_ge(s_ya, m * HY + c // 2)
                    sp.dma_start(rows[:, 5 * y:c, :], ysl[:, y % 2, :, :]).then_inc(s_yd[y % 2], 16)

            def loads(q, s, k):
                sp.dma_start(keep[:, k, :], keep_d[bass.ds(s * SC, SC)][None, :].to_broadcast([AW, SC])
                             ).then_inc(s_keep[k], 16)
                if q == MLP:
                    sp.dma_start(axe[:, k, :, :],
                                 spread[bass.ds(s * SC, SC), :].rearrange("(p g) d -> p g d", g=G)
                                 ).then_inc(s_axe[k], 16)
                    sp.dma_start(typb[D:AW, k, :], typ_d[bass.ds(s * SC, SC)][None, :].to_broadcast([T, SC])
                                 ).then_inc(s_axe[k], 16)

            def edge_pass(q):
                if q == MLP:
                    sp.wait_ge(s_scat, 16 * J)
                for k in range(K):
                    since(sp, s_keep[k], 16 * KEEPF * q)
                    loads(q, k, k)

                def step(s, i, k, live):
                    sp.wait_ge(s_evac, q * NS + s + 1)
                    sp.dma_start(scans[bass.ds(s * SC, SC), :].rearrange("(p g) d -> p g d", g=G),
                                 dmp[:, k, :, :]).then_inc(s_dump[k], 16)
                    loads(q, s + K, k)
                steps(sp, NI, K, step)

            table(0, ws)
            edge_pass(0)
            table(1, ws)
            edge_pass(1)
            for k in range(K):
                sp.wait_ge(s_axe[k], 32 * KEEPF)
            table(2, hs)
            edge_pass(2)
            typed_table(0)
            edge_pass(3)
            typed_table(1)
            edge_pass(4)
            sp.wait_ge(s_fin, 1)
            sp.dma_start(out.rearrange("(p j) d -> p j d", j=J), ws[0:N // J, :, :]).then_inc(s_out, 16)
            for k in range(K):
                sp.wait_ge(s_dump[k], 16 * NI * NPASS)
                sp.wait_ge(s_keep[k], 16 * KEEPF * NPASS)
            sp.wait_ge(s_out, 16)

        @block.gpsimd
        def _(pool):
            nc.gpsimd.memset(zero[:, :], 0.0)
            for b in bd.values():
                nc.gpsimd.memset(b[:, :], 0.0)
            for w in wz:
                nc.gpsimd.memset(w[:, :, :], 0.0)
            nc.gpsimd.memset(src_i[:, NCH:], 0)
            nc.gpsimd.memset(srct_i[:, NCH:], 0).then_inc(s_zs, 1)
            loose = {"allow_small_or_imprecise_dtypes": True}
            nc.gpsimd.iota(iota_hi[:, :, :], [[1, P], [0, HB]], base=0, channel_multiplier=0, **loose)
            nc.gpsimd.iota(iota_lo[:, :, :], [[1, J], [0, HB]], base=0, channel_multiplier=0, **loose)
            nc.gpsimd.iota(iota_lt[:, :, :], [[1, J * T], [0, G]], base=0, channel_multiplier=0, **loose)
            nc.gpsimd.iota(nid[:, :], [[1, J]], base=EP, channel_multiplier=J, **loose)
            nc.gpsimd.iota(typc[:, :], [[0, 1]], base=-D, channel_multiplier=1, **loose)
            nc.gpsimd.memset(ones[:, :], 1.0)
            nc.gpsimd.memset(ident[:, :], 0.0)
            nc.gpsimd.memset(lower[:, :], 0.0).then_inc(s_const, 1)
            pool.wait_ge(s_const, 1)
            nc.gpsimd.affine_select(out=ident[:, :], in_=ident[:, :], compare_op=ALU.not_equal, fill=1.0,
                                    base=0, pattern=[[-1, P]], channel_multiplier=1)
            nc.gpsimd.affine_select(out=lower[:, :], in_=lower[:, :], compare_op=ALU.is_ge, fill=1.0,
                                    base=0, pattern=[[-1, P]], channel_multiplier=1).then_inc(s_const, 1)

            def edge_pass(q):
                table = tab if q < 3 else ytab
                if q < 3:
                    pool.wait_ge(s_tab, 16 * (q + 1))
                else:
                    for y in range(2):
                        pool.wait_ge(s_yd[y], 16 * NG * (q - 2))

                def step(s, i, k, live):
                    pool.wait_ge(s_idx, q * IDXF + s + 1)
                    since(pool, s_turn, q * NS + s - (K - 1))
                    pool.sem_inc(s_go_pool, 1)
                    for g in range(G):
                        nc.gpsimd.indirect_dma_start(gat[:, k, g, :], None, table[:, :],
                                                     bass.IndirectOffsetOnAxis(ap=idx[:, k, g:g + 1], axis=0)
                                                     ).then_inc(s_gat[k], 16)
                steps(pool, NI, K, step)
                for k in range(K):
                    pool.wait_ge(s_dump[k], 16 * NI * (q + 1))
                if q == 0:
                    pool.wait_ge(s_endi, 1)
                for j in range(J):
                    nc.gpsimd.indirect_dma_start(es[:, j, :], None, scans[:, :],
                                                 bass.IndirectOffsetOnAxis(ap=end_i[:, j:j + 1], axis=0)
                                                 ).then_inc(s_ends, 16)
            edge_pass(0)
            pool.wait_ge(s_sprd, 1)
            pool.wait_ge(s_zero, 16 * zero_parts)
            for j in range(J):
                nc.gpsimd.indirect_dma_start(spread[:, :], bass.IndirectOffsetOnAxis(ap=start_i[:, j:j + 1], axis=0),
                                             ax[:, j, :], None).then_inc(s_scat, 16)
            for q in range(1, NPASS):
                edge_pass(q)

        @block.scalar
        def _(act):
            act.wait_ge(s_zs, 1)
            for z in range(zero_parts):
                r = min(zero_per, zero_rows - z * zero_per)
                act.dma_start(spread[z * zero_per:z * zero_per + r, :].rearrange("(p r) d -> p (r d)", p=P),
                              zero[:, 0:r // P * AW]).then_inc(s_zero, 16)

            def root(n):
                act.wait_ge(s_sq, n + 1)
                nc.scalar.activation(st[1][:, :], st[0][:, :], ACT.Sqrt).then_inc(s_rt, 1)

            def keep_transposed(c):
                act.wait_ge(s_lt, c + 1)
                since(act, s_lm, c - 1)
                nc.scalar.copy(tsl[:, c % 2, :], wide(c % 2)).then_inc(s_lc, 1)

            def product(n):
                for g in range(NG):
                    keep_transposed(n * NG + g)

            def typed(n, m):
                for g in range(NG):
                    keep_transposed(n * NG + g)
                    for j in range(g * JG + 1, g * JG + JG, 2):
                        act.wait_ge(s_ym, m * J + j + 1)
                        y = j // 5
                        since(act, s_yd[y % 2], 16 * (m * NG + y // 2))
                        nc.scalar.copy(ysl[:, y % 2, j % 5, :], bank(4 + j % 4)).then_inc(s_ya, 1)

            def edge_pass(q):
                lag = 2 if q == MLP else 1

                def step(s, i, k, live):
                    if q == MLP and live(0):
                        act.wait_ge(s_hsum, s + 1)
                        nc.scalar.activation(hsm[0:D, k % 2, :], hsm[0:D, k % 2, :], ACT.Relu).then_inc(s_relu, 1)
                    if q == MLP and live(1):
                        b = (k - 1) % 2
                        act.wait_ge(s_mlp, s)
                        since(act, s_scan, q * NS + s - 2)
                        nc.scalar.activation(zed[0:D, b, :], bank(6)[0:D, :], ACT.Relu,
                                             bias=eb2[:, 0:1]).then_inc(s_zed, 1)
                        act.wait_ge(s_wsum, s)
                        nc.scalar.copy(inv_s[:, bass.ds((s - 1) * G, G)], bank(7, G)).then_inc(s_wev, 1)
                    if live(lag):
                        i1, k1 = lagged(i, k, lag)
                        act.wait_ge(s_back, q * NS + s - lag + 1)
                        since(act, s_dump[k1], 16 * (q * NI + i1))
                        nc.scalar.copy(dmp[:, k1, :, :].rearrange("p g d -> p (g d)"),
                                       bank(2 + k1 % 2, G * D)).then_inc(s_evac, 1)
                steps(act, NI, K, step, lag)

            root(0)
            root(1)
            act.wait_ge(s_w, 16 * n_w)
            edge_pass(0)
            root(2)
            product(0)
            act.wait_ge(s_gi, 1)
            nc.scalar.activation(hs[:, :, :], hs[:, :, :], ACT.Gelu).then_inc(s_go, 1)
            product(1)
            root(3)
            product(2)
            product(3)
            edge_pass(1)
            root(4)
            product(4)
            edge_pass(2)
            product(5)
            root(5)
            typed(6, 0)
            product(7)
            edge_pass(3)
            typed(8, 1)
            product(9)
            edge_pass(4)
            act.wait_ge(s_zero, 16 * zero_parts)

        @block.vector
        def _(dve):
            v = nc.vector
            chained, roots, lins = [0], [0], [0]

            def link(ins):
                chained[0] += 1
                ins.then_inc(s_v, 1)
                dve.wait_ge(s_v, chained[0])

            def rsqrt(result, made):
                made.then_inc(s_sq, 1)
                roots[0] += 1
                dve.wait_ge(s_rt, roots[0])
                link(v.reciprocal(result, st[1][:, :]))

            def cols(a, w=D):
                return a.unsqueeze(2).to_broadcast([P, J, w])

            def rows(a, n=J):
                return a[:, :].unsqueeze(1).to_broadcast([P, n, D])

            def layernorm(last):
                link(v.tensor_reduce(out=st[0][:, :], in_=xs[:, :, :], axis=AX.X, op=ALU.add))
                link(v.tensor_scalar(st[2][:, :], st[0][:, :], 1.0 / D, None, ALU.mult))
                link(v.tensor_tensor(hs[:, :, :], xs[:, :, :], cols(st[2][:, :]), ALU.subtract))
                link(v.tensor_tensor(ws[:, :, :], hs[:, :, :], hs[:, :, :], ALU.mult))
                link(v.tensor_reduce(out=st[0][:, :], in_=ws[:, :, :], axis=AX.X, op=ALU.add))
                rsqrt(st[2][:, :], v.tensor_scalar(st[0][:, :], st[0][:, :], 1.0 / D, EPS, ALU.mult, ALU.add))
                last(v.scalar_tensor_tensor(out=hs[:, :, :], in0=hs[:, :, :], scalar=0.0,
                                            in1=cols(st[2][:, :]), op0=ALU.max, op1=ALU.mult))

            def features(ins):
                ins.then_inc(s_lin, 1)

            def product(n, write, first=None):
                for g in range(NG):
                    o = plain_before(n) * NG + g
                    dve.wait_ge(s_lm, n * NG + g + 1)
                    write(slice(g * JG, g * JG + JG), wide(2 + o % 2).rearrange("p (j d) -> p j d", d=D)
                          ).then_inc(s_le, 1)
                dve.wait_ge(s_le, (plain_before(n) + 1) * NG)

            def typed(n, m):
                for g in range(NG):
                    for j in range(g * JG, g * JG + JG, 2):
                        dve.wait_ge(s_ym, m * J + j + 1)
                        y = j // 5
                        since(dve, s_yd[y % 2], 16 * (m * NG + y // 2))
                        v.tensor_copy(ysl[:, y % 2, j % 5, :], bank(4 + j % 4)).then_inc(s_yv, 1)

            def split(f, q, r):
                link(v.tensor_scalar(q, f, 1.0 / J, -(J - 1) / (2.0 * J), ALU.mult, ALU.add))
                link(v.tensor_scalar(q, q, ROUND, None, ALU.add))
                link(v.tensor_scalar(q, q, ROUND, None, ALU.subtract))
                link(v.scalar_tensor_tensor(out=r, in0=q, scalar=-float(J), in1=f, op0=ALU.mult, op1=ALU.add))

            dve.wait_ge(s_row, 80)
            v.tensor_tensor(keep_r, row_d.bitcast(i32), row_p.bitcast(i32), ALU.is_equal)
            v.tensor_copy(typ_r, row_t.bitcast(i32)).then_inc(s_flag, 1)

            dve.wait_ge(s_edge, 16)
            link(v.tensor_copy(fa, src_i[:, 0:NCH]))
            split(fa, fb, lo_s[:, :])
            link(v.tensor_copy(hi_s[:, :], fb))
            v.scalar_tensor_tensor(out=srct_i[:, 0:NCH], in0=fa, scalar=float(T), in1=typ_e.bitcast(i32),
                                   op0=ALU.mult, op1=ALU.add)
            link(v.memset(odeg[:, :], 0.0))
            dve.wait_ge(s_const, 2)

            def count_sources(s, i, k, live):
                if live(0):
                    b = k % 2
                    since(dve, s_hist, s - 1)
                    for rows_, ids, vals, w in ((oh[:, b, :, :], iota_hi, hi_s, P), (ol[:, b, :, :], iota_lo, lo_s, J)):
                        last = v.tensor_tensor(rows_, ids[:, :, :],
                                               vals[:, bass.ds(s * HB, HB)].unsqueeze(1).to_broadcast([P, w, HB]),
                                               ALU.is_equal)
                    last.then_inc(s_oh, 1)
                if live(1):
                    dve.wait_ge(s_hist, s)
                    since(dve, s_histr, s - 1)
                    v.tensor_tensor(odeg[:, :], odeg[:, :], bank((k - 1) % 2, J), ALU.add).then_inc(s_histr, 1)
            steps(dve, NHB // 2, 2, count_sources, 1)
            dve.wait_ge(s_histr, NHB)

            rsqrt(odeg[:, :], v.tensor_scalar(st[0][:, :], odeg[:, :], 1.0, None, ALU.max))
            dve.wait_ge(s_x, 16)
            layernorm(link)
            v.tensor_tensor(ws[:, :, :], hs[:, :, :], cols(odeg[:, :]), ALU.mult).then_inc(s_tabrdy, 1)

            def fill_index(q):
                v.tensor_copy(idx[:, :, :].rearrange("p k g -> p (k g)"), idx_tab[q][:, 0:K * G]).then_inc(s_idx, K)
            fill_index(0)

            link(v.tensor_copy(fa, dst_e.bitcast(i32)))
            split(fa, fb, fa)
            v.tensor_copy(hi_s[:, :], fb)
            link(v.scalar_tensor_tensor(out=lo_s[:, :], in0=fa, scalar=float(T), in1=typ_e.bitcast(i32),
                                        op0=ALU.mult, op1=ALU.add))
            link(v.memset(cnt[:, :, :], 0.0))

            dve.wait_ge(s_w, 16 * n_w)
            dve.wait_ge(s_rowd, 64)
            link(v.tensor_tensor(bd["ea"][:, :], bd["ea"][:, :], bd["eb"][:, :], ALU.subtract))
            for n in range(2):
                for b in range(NB):
                    last = v.tensor_tensor(wprod[:, :, b, :], bas[n][:, b, :].unsqueeze(1).to_broadcast([P, T, D]),
                                           com[n][:, :, b:b + 1].to_broadcast([P, T, D]), ALU.mult)
                link(last)
                for h in range(2):
                    half = slice(D * h, D * h + D)
                    last = v.tensor_reduce(out=wz[n][half, h, :].rearrange("p (t o) -> p t o", t=T),
                                           in_=wprod[half, :, :, :].rearrange("p t b o -> p t o b"),
                                           axis=AX.X, op=ALU.add)
                link(last)

            def edge_pass(q):
                scale = wgt_tab[q]
                link(v.memset(scn[:, 1, SC - 1:SC], 0.0))
                if q == MLP:
                    link(v.memset(fil[0:AW, 1, SC - 1:SC], 0.0))

                def step(s, i, k, live):
                    b = k % 2
                    if live(0):
                        dve.wait_ge(s_gat[k], 16 * G * (q * NI + i + 1))
                        v.tensor_copy(idx[:, k, :], idx_tab[q][:, bass.ds((s + K) * G, G)]).then_inc(s_idx, 1)
                        if scale is not None:
                            v.tensor_tensor(gat[:, k, :, :], gat[:, k, :, :],
                                            scale[:, bass.ds(s * G, G)].unsqueeze(2).to_broadcast([P, G, D]),
                                            ALU.mult).then_inc(s_scl, 1)
                    if q == 0 and live(0):
                        since(dve, s_cc, s - 1)
                        v.tensor_tensor(oh[:, b, :, 0:G], iota_hi[:, :, 0:G],
                                        hi_s[:, bass.ds(s * G, G)].unsqueeze(1).to_broadcast([P, P, G]),
                                        ALU.is_equal)
                        v.tensor_tensor(olt[:, b, :, :], iota_lt[:, :, :],
                                        lo_s[:, bass.ds(s * G, G)].unsqueeze(1).to_broadcast([P, J * T, G]),
                                        ALU.is_equal).then_inc(s_coh, 1)
                    if q == MLP and live(0):
                        dve.wait_ge(s_turn, q * NS + s + 1)
                        dve.wait_ge(s_keep[k], 16 * (q * KEEPF + i + 1))
                        since(dve, s_fil, s)
                        v.tensor_tensor_scan(fil[0:AW, b, :], keep[:, k, :], bank(4 + b)[0:AW, :],
                                             fil[0:AW, 1 - b, SC - 1:SC], ALU.mult, ALU.add).then_inc(s_fil, 1)
                        dve.wait_ge(s_fil, s + 1)
                        since(dve, s_mlp, s - 1)
                        v.tensor_tensor(hsm[0:D, b, :], bank(b)[0:D, :], fil[0:D, b, :], ALU.add).then_inc(s_hsum, 1)
                        dve.wait_ge(s_axe[k], 32 * (i + 1))
                        since(dve, s_wsum, s - 1)
                        v.scalar_tensor_tensor(out=tpr[D:AW, b, :], in0=typb[D:AW, k, :], scalar=typc[D:AW, 0:1],
                                               in1=fil[D:AW, b, :], op0=ALU.is_equal, op1=ALU.mult
                                               ).then_inc(s_tpr, 1)
                    if q == 0 and live(1):
                        dve.wait_ge(s_cc, s)
                        since(dve, s_ccr, s - 1)
                        c = cnt[:, :, :].rearrange("p j t -> p (j t)")
                        v.tensor_tensor(c, c, bank(4 + (1 - b), J * T), ALU.add).then_inc(s_ccr, 1)
                    if live(1):
                        i1, k1 = lagged(i, k, 1)
                        if q == MLP:
                            dve.wait_ge(s_zed, s)
                            values, op = zed[0:D, 1 - b, :], ALU.max
                        else:
                            dve.wait_ge(s_turn, q * NS + s)
                            dve.wait_ge(s_keep[k1], 16 * (q * KEEPF + i1 + 1))
                            values, op = bank(1 - b)[0:D, :], ALU.add
                        since(dve, s_scan, q * NS + s - 1)
                        since(dve, s_back, q * NS + s - 2)
                        v.tensor_tensor_scan(scn[:, 1 - b, :], keep[0:D, k1, :], values,
                                             scn[:, b, SC - 1:SC], ALU.mult, op).then_inc(s_scan, 1)
                steps(dve, NI, K, step, 1)

            def pass_ends(q):
                dve.wait_ge(s_ends, 16 * J * (q + 1))

            edge_pass(0)
            dve.wait_ge(s_ccr, NS)
            link(v.tensor_reduce(out=deg[:, :], in_=cnt[:, :, :], axis=AX.X, op=ALU.add))
            v.tensor_tensor_scan(csum[:, :], ones[:, :], deg[:, :], 0.0, ALU.mult, ALU.add).then_inc(s_tot, 1)
            link(v.tensor_scalar(dmask[:, :], deg[:, :], 1.0, None, ALU.min))
            dve.wait_ge(s_pre, 1)
            link(v.tensor_copy(pre[:, :], bank(6, 1)))
            link(v.tensor_scalar(csum[:, :], csum[:, :], pre[:, 0:1], None, ALU.add))
            v.tensor_scalar(end_i[:, :], csum[:, :], -1.0, 0.0, ALU.add, ALU.max).then_inc(s_endi, 1)
            link(v.tensor_tensor(st[2][:, :], csum[:, :], deg[:, :], ALU.subtract))
            link(v.tensor_tensor(st[2][:, :], st[2][:, :], nid[:, :], ALU.subtract))
            link(v.tensor_tensor(st[2][:, :], st[2][:, :], dmask[:, :], ALU.mult))
            link(v.tensor_tensor(start_i[:, :], st[2][:, :], nid[:, :], ALU.add))
            rsqrt(gcnf[:, :], v.tensor_scalar(st[0][:, :], deg[:, :], 1.0, None, ALU.max))
            link(v.tensor_tensor(gcnf[:, :], gcnf[:, :], dmask[:, :], ALU.mult))
            link(v.reciprocal(meanf[:, :], st[0][:, :]))
            link(v.tensor_tensor(meanf[:, :], meanf[:, :], dmask[:, :], ALU.mult))
            link(v.tensor_scalar(cnt[:, :, :], cnt[:, :, :], 1.0, None, ALU.max))
            link(v.reciprocal(ax[:, :, D:AW], cnt[:, :, :]))
            link(v.tensor_tensor(xs[:, :, :], xs[:, :, :], rows(bias["g2"]), ALU.add))
            pass_ends(0)
            features(v.tensor_tensor(ws[:, :, :], es[:, :, :], cols(gcnf[:, :]), ALU.mult))
            product(0, lambda c, o: v.tensor_tensor(hs[:, c, :], o, rows(bias["g1"], JG), ALU.add))
            dve.sem_inc(s_gi, 1)
            dve.wait_ge(s_go, 1)
            dve.sem_inc(s_lin, 1)
            product(1, lambda c, o: v.tensor_tensor(xs[:, c, :], o, xs[:, c, :], ALU.add))

            layernorm(features)
            product(2, lambda c, o: v.tensor_tensor(ax[:, c, 0:D], o, rows(bias["ea"], JG), ALU.add))
            dve.sem_inc(s_sprd, 1)
            dve.sem_inc(s_lin, 1)
            product(3, lambda c, o: v.tensor_copy(ws[:, c, :], o))
            dve.sem_inc(s_tabrdy, 1)
            fill_index(1)
            edge_pass(1)
            pass_ends(1)
            link(v.tensor_tensor(es[:, :, :], es[:, :, :], cols(dmask[:, :]), ALU.mult))
            link(v.tensor_tensor(xs[:, :, :], xs[:, :, :], es[:, :, :], ALU.add))

            layernorm(lambda ins: ins.then_inc(s_tabrdy, 1))
            fill_index(2)
            dve.wait_ge(s_tabrdy, 3)
            dve.sem_inc(s_lin, 1)
            product(4, lambda c, o: v.tensor_tensor(rs[:, c, :], o, rows(bias["sf"], JG), ALU.add))
            link(v.tensor_tensor(xs[:, :, :], xs[:, :, :], rs[:, :, :], ALU.add))
            link(v.tensor_tensor(xs[:, :, :], xs[:, :, :], rows(bias["ng"]), ALU.add))
            edge_pass(2)
            pass_ends(2)
            features(v.tensor_tensor(ws[:, :, :], es[:, :, :], cols(meanf[:, :]), ALU.mult))
            product(5, lambda c, o: v.tensor_tensor(xs[:, c, :], o, xs[:, c, :], ALU.add))

            layernorm(features)
            typed(6, 0)
            fill_index(3)
            dve.sem_inc(s_lin, 1)
            product(7, lambda c, o: v.tensor_tensor(rs[:, c, :], o, rows(bias["r1"], JG), ALU.add))
            edge_pass(3)
            pass_ends(3)
            link(v.tensor_tensor(es[:, :, :], es[:, :, :], cols(dmask[:, :]), ALU.mult))
            link(v.tensor_tensor(es[:, :, :], es[:, :, :], rs[:, :, :], ALU.add))

            features(v.tensor_scalar(hs[:, :, :], es[:, :, :], 0.0, None, ALU.max))
            typed(8, 1)
            fill_index(4)
            dve.sem_inc(s_lin, 1)
            product(9, lambda c, o: v.tensor_tensor(rs[:, c, :], o, rows(bias["r2"], JG), ALU.add))
            link(v.tensor_tensor(xs[:, :, :], xs[:, :, :], rs[:, :, :], ALU.add))
            edge_pass(4)
            pass_ends(4)
            link(v.tensor_tensor(es[:, :, :], es[:, :, :], cols(dmask[:, :]), ALU.mult))
            v.tensor_tensor(ws[:, :, :], es[:, :, :], xs[:, :, :], ALU.add).then_inc(s_fin, 1)

        @block.tensor
        def _(pe):
            pe.wait_ge(s_const, 2)

            def count_sources(s, i, k, live):
                b = k % 2
                pe.wait_ge(s_oh, s + 1)
                since(pe, s_histr, s - 1)
                for c in range(HB):
                    last = nc.tensor.matmul(bank(b, J), oh[:, b, :, c], ol[:, b, :, c],
                                            start=(c == 0), stop=(c == HB - 1))
                last.then_inc(s_hist, 1)
            steps(pe, NHB // 2, 2, count_sources)

            def transpose_group(rows, n, g):
                c = n * NG + g
                since(pe, s_lc, c - 1)
                for q in range(JG // 2):
                    last = nc.tensor.transpose(wide(c % 2)[:, q * P:q * P + P],
                                               rows[:, g * JG + 2 * q:g * JG + 2 * q + 2, :].rearrange("p j d -> p (j d)"),
                                               ident[:, :])
                last.then_inc(s_lt, 1)

            def product(n, rows):
                w = bd[LIN[n]]
                pe.wait_ge(s_lin, n + 1)
                for g in range(NG + 1):
                    if g < NG:
                        transpose_group(rows, n, g)
                    if g > 0:
                        c = n * NG + g - 1
                        o = plain_before(n) * NG + g - 1
                        pe.wait_ge(s_lc, c + 1)
                        since(pe, s_le, o - 1)
                        for q in range(JG // 2):
                            last = nc.tensor.matmul(wide(2 + o % 2)[:, q * P:q * P + P],
                                                    tsl[:, c % 2, q * P:q * P + P], w[:, :], start=True, stop=True)
                        last.then_inc(s_lm, 1)

            def typed(n, m, rows):
                pe.wait_ge(s_lin, n + 1)
                for g in range(NG):
                    c = n * NG + g
                    transpose_group(rows, n, g)
                    pe.wait_ge(s_lc, c + 1)
                    for j in range(g * JG, g * JG + JG):
                        if j >= 4:
                            pe.wait_ge(s_yv if j % 2 == 0 else s_ya, m * HY + (j - 4) // 2 + 1)
                        q = (j - g * JG) // 2
                        last = nc.tensor.matmul(bank(4 + j % 4), tsl[:, c % 2, q * P:q * P + P],
                                                wz[m][:, j % 2, :], start=True, stop=True)
                        last.then_inc(s_ym, 1)
                    pe.wait_ge(s_ym, m * J + g * JG + JG)
                    pe.sem_inc(s_lm, 1)

            def edge_pass(q):
                mlp = q == MLP
                lag = 2 if mlp else 1
                scaled = sum(w is not None for w in wgt_tab[:q])

                def by_edge(a, g):
                    return a.rearrange("d (p g) -> d g p", g=G)[:, g, :]

                def step(s, i, k, live):
                    b = k % 2
                    if live(0):
                        if wgt_tab[q] is not None:
                            pe.wait_ge(s_scl, scaled * NS + s + 1)
                        else:
                            pe.wait_ge(s_gat[k], 16 * G * (q * NI + i + 1))
                        if mlp:
                            since(pe, s_hsum, s - 1)
                        else:
                            since(pe, s_scan, q * NS + s - 1)
                        pe.sem_inc(s_go_pe, 1)
                        for g in range(G):
                            last = nc.tensor.transpose(by_edge(bank(b)[0:D, :], g), gat[:, k, g, :], ident[:, :])
                        if mlp:
                            pe.wait_ge(s_axe[k], 32 * (i + 1))
                            since(pe, s_tpr, s - 1)
                            pe.sem_inc(s_go_pe, 1)
                            for g in range(G):
                                last = nc.tensor.transpose(by_edge(bank(4 + b)[0:AW, :], g), axe[:, k, g, :],
                                                           ident[:, :])
                        last.then_inc(s_turn, 1)
                    if q == 0 and live(0):
                        pe.wait_ge(s_coh, s + 1)
                        since(pe, s_ccr, s - 1)
                        for g in range(G):
                            last = nc.tensor.matmul(bank(4 + b, J * T), oh[:, b, :, g], olt[:, b, :, g],
                                                    start=(g == 0), stop=(g == G - 1))
                        last.then_inc(s_cc, 1)
                    if mlp and live(1):
                        pe.wait_ge(s_relu, s)
                        since(pe, s_zed, s - 1)
                        pe.sem_inc(s_go_pe, 1)
                        nc.tensor.matmul(bank(6)[0:D, :], ew2[:, :], hsm[0:D, 1 - b, :],
                                         start=True, stop=True).then_inc(s_mlp, 1)
                        pe.wait_ge(s_tpr, s)
                        since(pe, s_wev, s - 1)
                        for g in range(G):
                            last = nc.tensor.matmul(bank(7)[:, g:g + 1], by_edge(tpr[D:AW, 1 - b, :], g),
                                                    ones[D:AW, 0:1], start=True, stop=True)
                        last.then_inc(s_wsum, 1)
                    if live(lag):
                        b1 = (k - lag) % 2
                        pe.wait_ge(s_scan, q * NS + s - lag + 1)
                        since(pe, s_evac, q * NS + s - lag - 1)
                        pe.sem_inc(s_go_pe, 1)
                        for g in range(G):
                            last = nc.tensor.transpose(bank(2 + b1)[:, g * D:g * D + D],
                                                       by_edge(scn[:, b1, :], g), ident[0:D, 0:D])
                        last.then_inc(s_back, 1)
                steps(pe, NI, K, step, lag)

            edge_pass(0)
            pe.wait_ge(s_tot, 1)
            nc.tensor.matmul(bank(6, 1), lower[:, :], csum[:, J - 1:J], start=True, stop=True).then_inc(s_pre, 1)
            product(0, ws)
            product(1, hs)
            product(2, hs)
            product(3, hs)
            pe.wait_ge(s_le, NG * plain_before(4))
            edge_pass(1)
            product(4, hs)
            pe.wait_ge(s_le, NG * plain_before(5))
            edge_pass(2)
            product(5, ws)
            typed(6, 0, hs)
            pe.wait_ge(s_yv, HY)
            pe.wait_ge(s_ya, HY)
            product(7, hs)
            pe.wait_ge(s_le, NG * plain_before(8))
            edge_pass(3)
            typed(8, 1, hs)
            pe.wait_ge(s_yv, 2 * HY)
            pe.wait_ge(s_ya, 2 * HY)
            product(9, hs)
            pe.wait_ge(s_le, NG * plain_before(10))
            edge_pass(4)


def kernel(**inputs):
    import numpy as _np
    import concourse.bacc as _bacc
    from concourse import mybir as _mybir
    from concourse.bass_utils import run_bass_kernel_spmd as _run

    a = {k: _np.asarray(v) for k, v in inputs.items()}

    def pad(row, value):
        return _np.concatenate([row, _np.full(EP - E, value, row.dtype)])

    def by_superchunk(row):
        return _np.ascontiguousarray(row.reshape(NS, P, G).transpose(1, 0, 2).reshape(P, NCH))

    dst = pad(a["dst"], NPAD - 1)
    src = pad(a["src"], NPAD - 1)
    typ = pad(a["edge_type_8"], 0)
    before = _np.concatenate([_np.full(1, -1, dst.dtype), dst[:-1]])
    x = _np.concatenate([a["x"], _np.zeros((NPAD - N, D), a["x"].dtype)])
    data = [
        ("x", x), ("src", by_superchunk(src)), ("dst", by_superchunk(dst)), ("typ", by_superchunk(typ)),
        ("wgt", by_superchunk(pad(a["edge_weight"], 0))),
        ("dst_row", dst.reshape(P, NCH)), ("prev_row", before.reshape(P, NCH)), ("typ_row", typ.reshape(P, NCH)),
        ("gcn_w1", a["L0_gnn_w1"]), ("gcn_b1", a["L0_gnn_b1"]), ("gcn_w2", a["L0_gnn_w2"]), ("gcn_b2", a["L0_gnn_b2"]),
        ("edge_w1", a["L1_gnn_W1"]), ("edge_b1", a["L1_gnn_b1"]), ("edge_w2", a["L1_gnn_W2"]), ("edge_b2", a["L1_gnn_b2"]),
        ("self_wT", a["L2_gnn_W_self"].T), ("self_b", a["L2_gnn_b_self"]),
        ("neigh_wT", a["L2_gnn_W_neigh"].T), ("neigh_b", a["L2_gnn_b_neigh"]),
        ("basis1", a["L3_gnn_basis1"]), ("comp1", a["L3_gnn_comp1"]), ("root1", a["L3_gnn_root1"]), ("bias1", a["L3_gnn_bias1"]),
        ("basis2", a["L3_gnn_basis2"]), ("comp2", a["L3_gnn_comp2"]), ("root2", a["L3_gnn_root2"]), ("bias2", a["L3_gnn_bias2"]),
    ]
    nc = _bacc.Bacc("TRN2", target_bir_lowering=False, num_devices=1)
    arrays, args = {}, []
    for name, value in data:
        arrays[f"in_{name}"] = _np.ascontiguousarray(value)
        args.append(nc.dram_tensor(f"in_{name}", value.shape, _mybir.dt.from_np(value.dtype), kind="ExternalInput").ap())
    out = nc.dram_tensor("out_0", (N, D), _mybir.dt.float32, kind="ExternalOutput").ap()
    gnn_kernel(nc, *args, out)
    r = _run(nc, [arrays], core_ids=[0])
    return r.results[0]["out_0"]
```

```python
import concourse.bass as bass
from concourse import mybir
from contextlib import ExitStack

N = 6250
E = 200000
D = 64
T = 8
NB = 4
P = 128
J = 50
NPAD = P * J
ST = 2
GH = 2
G = ST * GH
SH = P * GH
SC = ST * SH
K = 4
NI = -(-E // (SC * K))
NS = NI * K
EP = NS * SC
EH = EP // ST
NCH = NS * G
AW = D + T
JG = 10
NG = J // JG
HB = 16
NHB = NCH // HB
PEEL = 2
EPS = 1e-5
ROUND = 1.5 * 2.0 ** 23


def gnn_kernel(nc, x, src, dst, typ, wgt, dst_row, prev_row, typ_row,
               gcn_w1, gcn_b1, gcn_w2, gcn_b2,
               edge_w1, edge_b1, edge_w2, edge_b2,
               self_wT, self_b, neigh_wT, neigh_b,
               basis1, comp1, root1, bias1, basis2, comp2, root2, bias2, out):
    f32, f16, bf16, i32 = mybir.dt.float32, mybir.dt.float16, mybir.dt.bfloat16, mybir.dt.int32
    ALU = mybir.AluOpType
    ACT = mybir.ActivationFunctionType
    AX = mybir.AxisListType

    tab = nc.dram_tensor("node_table", [NPAD, D], f32).ap()
    ytab = nc.dram_tensor("typed_table", [NPAD * T, D], f32).ap()
    spread = nc.dram_tensor("spread_table", [EP + NPAD, AW], f32).ap()
    scans = nc.dram_tensor("scan_rows", [EP, D], f32).ap()
    flags_d = nc.dram_tensor("keep_and_type_rows", [2, EP], bf16).ap()

    with ExitStack() as ctx:
        def sb(name, shape, dt=f32):
            return ctx.enter_context(nc.sbuf_tensor(name, shape, dt))

        def sem(name):
            return ctx.enter_context(nc.semaphore(name))

        src_i = sb("src_i", [P, NCH + K * G], i32)
        srct_i = sb("srct_i", [P, NCH + K * G], i32)
        wgt_s = sb("wgt_s", [P, NCH])
        inv_s = sb("inv_s", [P, NCH])
        hi_s = sb("hi_s", [P, NCH], f16)
        lo_s = sb("lo_s", [P, NCH], f16)

        xs = sb("xs", [P, J, D])
        hs = sb("hs", [P, J, D])
        ws = sb("ws", [P, J, D])
        es = sb("es", [P, J, D])
        rs = sb("rs", [P, J, D])
        ax = sb("ax", [P, J, AW])
        cnt = sb("cnt", [P, J, T])
        odeg = sb("odeg", [P, J])
        deg = sb("deg", [P, J])
        dmask = sb("dmask", [P, J])
        gcnf = sb("gcnf", [P, J])
        meanf = sb("meanf", [P, J])
        csum = sb("csum", [P, J])
        pre = sb("pre", [P, 1])
        st = [sb(f"st{n}", [P, J]) for n in range(3)]
        end_i = sb("end_i", [P, J], i32)
        start_i = sb("start_i", [P, J], i32)

        def part(t, n, w=NCH):
            return t[:, :, :].rearrange("p j d -> p (j d)")[:, n * w:n * w + w]

        dst_e, fa = part(es, 0), part(es, 1)
        fb, typ_e = part(rs, 0), part(rs, 1)
        row_d, row_p = part(ax, 0), part(ax, 1)

        ident = sb("ident", [P, P])
        lower = sb("lower", [P, P])
        iota_hi = sb("iota_hi", [P, P, HB], f16)
        iota_lo = sb("iota_lo", [P, J, HB], f16)
        iota_lt = sb("iota_lt", [P, J * T, G], f16)
        nid = sb("nid", [P, J])
        typc = sb("typc", [P, 1])
        pair = sb("pair", [P, ST])
        ones = sb("ones", [P, J])
        bd = {n: sb(f"bd_{n}", [P, P]) for n in ("g1", "g2", "ea", "eb", "sf", "ng", "r1", "r2", "w2")}
        bias = {n: sb(f"bias_{n}", [P, D]) for n in ("g1", "g2", "ea", "sf", "ng", "r1", "r2")}
        eb2 = sb("eb2", [P, 1])
        wz = [sb(f"wz{n}", [P, 2, T * D]) for n in range(2)]
        zrow = 28 * AW
        zero = sb("zero", [P, zrow])
        bas = [sb(f"bas{n}", [P, NB, D]) for n in range(2)]
        com = [sb(f"com{n}", [P, T, NB]) for n in range(2)]

        idx = sb("idx", [P, K, G], i32)
        gat = sb("gat", [P, K, GH, ST, D])
        flags = sb("flags", [P, 2, K, SH], bf16)
        keep = flags[:, 0, :, :]
        typb = flags[:, 1, :, :]
        dmp = sb("dmp", [P, K, ST, GH, D])
        scn = sb("scn", [P, 2, SH])
        cross = sb("cross", [P, J])
        mid = sb("mid", [P, D])
        share = sb("share", [P, JG, D])
        crow = [sb(f"crow{n}", [P, P]) for n in range(2)]
        oh = sb("oh", [P, 2, P, HB], f16)
        ol = sb("ol", [P, 2, J, HB], f16)
        olt = sb("olt", [P, 2, J * T, G], f16)
        tsl = sb("tsl", [P, 2, JG * D])

        cuts = [K * G * AW] + [2 * G * D] * 2 + [2 * SH] * 5
        shared = sb("shared", [P, max(sum(cuts), 2 * 5 * T * D)])
        at = [sum(cuts[:n]) for n in range(len(cuts))]
        axe = shared[:, 0:cuts[0]].rearrange("p (k t g d) -> p k t g d", k=K, t=ST, g=GH)
        axf, axl = (shared[:, a:a + c].rearrange("p (b g t d) -> p b g t d", b=2, g=GH, t=ST)
                    for a, c in zip(at[1:3], cuts[1:3]))
        fil, fit, tpr, hsm, zed = (shared[:, a:a + c].rearrange("p (b n) -> p b n", b=2)
                              for a, c in zip(at[3:], cuts[3:]))
        ysl = shared[:, 0:2 * 5 * T * D].rearrange("p (b j n) -> p b j n", b=2, j=5)
        wprod = shared[:, 0:T * NB * D].rearrange("p (t b o) -> p t b o", t=T, b=NB)
        row_t = shared[:, 0:NCH]
        keep_r = shared[:, NCH:NCH + NCH // 2].bitcast(bf16)
        typ_r = shared[:, 2 * NCH:2 * NCH + NCH // 2].bitcast(bf16)

        ps = ctx.enter_context(nc.psum_tensor("ps", [P, 8 * 512], f32))

        def bank(n, w=512):
            return ps[:, 512 * n:512 * n + w]

        def wide(n):
            return ps[:, 1024 * n:1024 * n + JG * D]

        s_edge = sem("edges_loaded")
        s_x = sem("x_loaded")
        s_row = sem("rows_loaded")
        s_w = sem("weights_loaded")
        s_const = sem("constants_made")
        s_zs = sem("zero_tiles_made")
        s_zero = sem("spread_table_zeroed")
        s_rowd = sem("flag_rows_written")
        s_flag = sem("flag_rows_made")
        s_v = sem("vector_chain")
        s_oh = sem("source_onehots_made")
        s_hist = sem("source_batches_counted")
        s_coh = sem("target_onehots_made")
        s_cc = sem("target_superchunks_counted")
        s_tabrdy = sem("table_values_ready")
        s_tab = sem("table_written")
        s_tot = sem("partition_totals_ready")
        s_pre = sem("partition_prefix_summed")
        s_endi = sem("end_index_ready")
        s_sprd = sem("spread_rows_ready")
        s_scat = sem("spread_rows_scattered")
        s_ends = [sem(f"end_rows_gathered{g}") for g in range(NG)]
        s_idx = sem("index_slots_filled")
        s_gat = [sem(f"rows_gathered{k}") for k in range(K)]
        s_scl = sem("rows_scaled")
        s_turn = sem("rows_transposed")
        s_scan = sem("superchunks_scanned")
        s_back = sem("scans_transposed_back")
        s_evac = sem("scan_rows_evacuated")
        s_dump = [sem(f"scan_rows_dumped{k}") for k in range(K)]
        s_keep = [sem(f"keep_loaded{h}") for h in range(K // 2)]
        s_axe = [sem(f"spread_rows_loaded{h}") for h in range(K // 2)]
        s_axc = sem("spread_rows_split")
        s_cross = sem("crossing_rows_masked")
        s_crs = sem("crossing_rows_summed")
        s_mid = sem("middle_row_loaded")
        s_fil = sem("target_rows_filled")
        s_hsum = sem("edge_hidden_summed")
        s_tpr = sem("type_products_made")
        s_relu = sem("edge_hidden_rectified")
        s_mlp = sem("edge_mlp_multiplied")
        s_zed = sem("edge_mlp_rectified")
        s_wsum = sem("inverse_counts_summed")
        s_wev = sem("inverse_counts_kept")
        s_lin = sem("node_features_ready")
        s_lt = sem("node_groups_transposed")
        s_lc = sem("node_transposes_copied")
        s_lm = sem("node_groups_multiplied")
        s_le = sem("node_products_read")
        s_ym = sem("typed_columns_multiplied")
        s_ya = sem("typed_columns_read")
        s_yd = [sem(f"typed_rows_written{k}") for k in range(2)]
        s_sq = sem("sqrt_input_ready")
        s_rt = sem("sqrt_done")
        s_iota = sem("first_iotas_made")
        s_cen = sem("gpsimd_chain")
        s_go = sem("gelu_done")
        s_go_pool = sem("gathers_begun")
        s_go_pe = sem("products_begun")
        s_go_sp = sem("flag_loads_begun")
        s_fin = sem("result_ready")
        s_out = sem("result_written")

        MLP = 1
        PADDED = [s for s in range(NS - K, NS) if EH + s * SH >= E]
        NPASS = 5
        idx_tab = [src_i, src_i, src_i, srct_i, srct_i]
        wgt_tab = [None, None, wgt_s, inv_s, inv_s]
        IDXF = NS + K
        ORDER_T, ORDER_M = [], []
        for t in range(NG + 2):
            for name, g in (("g1", t), ("g2", t - 1), ("ab", t - 2)):
                if 0 <= g < NG:
                    ORDER_T.append((name, g))
                    ORDER_M += [("ea", g), ("eb", g)] if name == "ab" else [(name, g)]
        ORDER_T += [("sf", g) for g in range(NG)]
        ORDER_M += [("sf", g) for g in range(NG)]
        for t in range(NG + 1):
            if t > 0:
                ORDER_T.append(("y0", t - 1))
            if t < NG:
                ORDER_T.append(("ng", t))
                ORDER_M.append(("ng", t))
            if t > 0:
                ORDER_M.append(("y0", t - 1))
        for name in ("r1", "y1", "r2"):
            ORDER_T += [(name, g) for g in range(NG)]
            ORDER_M += [(name, g) for g in range(NG)]
        BY_VECTOR = [key for key in ORDER_T if key[0] != "g2"]
        PLAIN = [key for key in ORDER_M if key[0] not in ("y0", "y1")]

        def product_slot(key):
            return 3 if key[0] in ("ng", "r1", "r2") else 2 + PLAIN.index(key) % 2

        def slot_read(key):
            before = [n for n, other in enumerate(PLAIN[:PLAIN.index(key)]) if product_slot(other) == product_slot(key)]
            return before[-1] + 1 if before else 0

        def features_used(c):
            if c < 2:
                return 0
            name, g = ORDER_T[c - 2]
            return ORDER_M.index(("eb" if name == "ab" else name, g)) + 1

        def plain_until(name):
            return max(n for n, key in enumerate(PLAIN) if key[0] == name) + 1

        def since(eng, semaphore, value):
            if not isinstance(value, int) or value > 0:
                eng.wait_ge(semaphore, value)

        def steps(eng, count, per, body, lag=0, tail=0):
            for i in range(PEEL):
                for k in range(per):
                    body(per * i + k, i, k, lambda n, s=per * i + k: s >= n)
            with eng.Fori(PEEL, count - tail) as i:
                for k in range(per):
                    body(i * per + k, i, k, lambda n: True)
            for i in range(count - tail, count):
                for k in range(per):
                    body(per * i + k, i, k, lambda n: True)
            for k in range(lag):
                body(per * count + k, count, k, lambda n, k=k: n > k)

        def is_at(s, unit):
            return isinstance(s, int) and s == unit

        def gathered(q, s, i, k):
            left_out = GH if NS - K + k in PADDED else 0
            return 16 * (G * (q * NI + i + 1) - left_out * (q + is_at(s, NS - K + k)))

        def lagged(i, k, lag):
            return (i if k >= lag else i - 1), (k - lag) % K

        zero_rows = EP + NPAD
        zero_per = zrow // AW * P
        zero_parts = -(-zero_rows // zero_per)
        n_w = 2 * len(bd) + len(bias) + 2 + 6 + 1

        block = ctx.enter_context(nc.Block())

        @block.sync
        def _(sp):
            sp.dma_start(src_i[:, 0:NCH], src).then_inc(s_edge, 16)
            sp.dma_start(xs[:, :, :], x.rearrange("(p j) d -> p j d", j=J)).then_inc(s_x, 16)
            sp.dma_start(row_d.bitcast(i32), dst_row).then_inc(s_row, 16)
            sp.dma_start(row_p.bitcast(i32), prev_row).then_inc(s_row, 16)
            sp.dma_start(row_t.bitcast(i32), typ_row).then_inc(s_row, 16)
            sp.dma_start(dst_e.bitcast(i32), dst).then_inc(s_row, 16)
            sp.dma_start(typ_e.bitcast(i32), typ).then_inc(s_row, 16)
            sp.wait_ge(s_flag, 1)
            for n, row in enumerate((keep_r, typ_r)):
                sp.dma_start(flags_d[n, :].rearrange("(p m) -> p m", p=P), row).then_inc(s_rowd, 16)
            sp.wait_ge(s_zs, 1)
            for n, (w, b) in {"g1": (gcn_w1, gcn_b1), "g2": (gcn_w2, gcn_b2),
                              "ea": (edge_w1[0:D, :], edge_b1), "eb": (edge_w1[D:2 * D, :], None),
                              "sf": (self_wT, self_b), "ng": (neigh_wT, neigh_b),
                              "r1": (root1, bias1), "r2": (root2, bias2), "w2": (edge_w2, None)}.items():
                sp.dma_start(bd[n][0:D, 0:D], w).then_inc(s_w, 16)
                sp.dma_start(bd[n][D:P, D:P], w).then_inc(s_w, 16)
                if b is not None:
                    sp.dma_start(bias[n][:, :], b[None, :].to_broadcast([P, D])).then_inc(s_w, 16)
            for h in range(ST):
                sp.dma_start(eb2[D * h:D * h + D, :], edge_b2[:, None]).then_inc(s_w, 16)
            for n, (ba, co) in enumerate(((basis1, comp1), (basis2, comp2))):
                for h in range(2):
                    sp.dma_start(bas[n][D * h:D * h + D, :, :], ba.rearrange("b i o -> i b o")).then_inc(s_w, 16)
                sp.dma_start(com[n][:, :, :], co[None, :, :].to_broadcast([P, T, NB])).then_inc(s_w, 16)
            sp.dma_start(wgt_s[:, :], wgt).then_inc(s_w, 16)
            sp.wait_ge(s_rowd, 32)

            def table(q, rows, parts):
                for g in range(parts):
                    c = slice(g * J // parts, (g + 1) * J // parts)
                    sp.wait_ge(s_tabrdy, 1 + (q - 1) * NG + g + 1 if q else 1)
                    sp.dma_start(tab.rearrange("(p j) d -> p j d", j=J)[:, c, :], rows[:, c, :]).then_inc(s_tab, 16)

            def typed_table(m):
                rows = ytab.rearrange("(p j t) d -> p j (t d)", j=J, t=T)
                for y in range(J // 5):
                    c = 5 * y + 5
                    sp.wait_ge(s_ya, m * J + c)
                    sp.dma_start(rows[:, 5 * y:c, :], ysl[:, y % 2, :, :]).then_inc(s_yd[y % 2], 16)

            def load_flags(q, s, h):
                n_rows = 2 if q == MLP else 1
                for n in range(ST):
                    row = flags_d[0:n_rows, bass.ds(n * EH + s * SH, 2 * SH)][None, :, :].to_broadcast([D, n_rows, 2 * SH])
                    sp.dma_start(flags[D * n:D * n + D, 0:n_rows, 2 * h:2 * h + 2, :].rearrange("d r k n -> d r (k n)"),
                                 row).then_inc(s_keep[h], 16)

            def load_spread(s, h):
                for n in range(ST):
                    rows = spread[bass.ds(n * EH + s * SH, 2 * SH), :]
                    sp.dma_start(axe[:, 2 * h:2 * h + 2, n, :, :].rearrange("p k g d -> p k (g d)"),
                                 rows.rearrange("(k p g) d -> p k (g d)", k=2, g=GH)).then_inc(s_axe[h], 16)

            def edge_pass(q):
                if q == MLP:
                    sp.wait_ge(s_scat, 16 * J)
                for h in range(K // 2):
                    load_flags(q, 2 * h, h)
                    if q == MLP:
                        load_spread(2 * h, h)

                def step(s, i, k, live, more=True):
                    if live(1):
                        k1 = (k - 1) % K
                        sp.wait_ge(s_evac, q * NS + s)
                        sp.dma_start(scans.rearrange("(t e) d -> t e d", t=ST)[:, bass.ds((s - 1) * SH, SH), :]
                                     .rearrange("t (p g) d -> p t (g d)", g=GH),
                                     dmp[:, k1, :, :, :].rearrange("p t g d -> p t (g d)")).then_inc(s_dump[k1], 16)
                    if k % 2 and more:
                        sp.wait_ge(s_scan, q * NS + s + 1)
                        sp.sem_inc(s_go_sp, 1)
                        load_flags(q, s - 1 + K, k // 2)
                    if k % 2 == 0 and more and q == MLP:
                        sp.wait_ge(s_axc, s + 2)
                        load_spread(s + K, k // 2)
                steps(sp, NI - 1, K, step)
                for k in range(K + 1):
                    step(NS - K + k, NI - 1, k, lambda n: True, False)
                for k in range(K):
                    sp.wait_ge(s_dump[k], 16 * NI * (q + 1))
                sp.dma_start(mid[:, :], scans[EH - 1:EH, :].to_broadcast([P, D])).then_inc(s_mid, 16)

            table(0, ws, 1)
            edge_pass(0)
            table(1, ws, NG)
            edge_pass(1)
            table(2, hs, NG)
            edge_pass(2)
            typed_table(0)
            edge_pass(3)
            typed_table(1)
            edge_pass(4)
            for g in range(NG):
                c = slice(g * JG, g * JG + JG)
                sp.wait_ge(s_fin, g + 1)
                sp.dma_start(out.rearrange("(p j) d -> p j d", j=J)[:, c, :], ws[0:N // J, c, :]).then_inc(s_out, 16)
            for h in range(K // 2):
                sp.wait_ge(s_keep[h], 32 * NI * NPASS)
            sp.wait_ge(s_out, 16 * NG)

        @block.gpsimd
        def _(pool):
            loose = {"allow_small_or_imprecise_dtypes": True}
            nc.gpsimd.iota(iota_hi[:, :, :], [[1, P], [0, HB]], base=0, channel_multiplier=0, **loose)
            nc.gpsimd.iota(iota_lo[:, :, :], [[1, J], [0, HB]], base=0, channel_multiplier=0, **loose).then_inc(s_iota, 1)
            nc.gpsimd.memset(zero[:, :], 0.0)
            for b in bd.values():
                nc.gpsimd.memset(b[:, :], 0.0)
            for w in wz:
                nc.gpsimd.memset(w[:, :, :], 0.0)
            nc.gpsimd.memset(src_i[:, NCH:], 0)
            nc.gpsimd.memset(srct_i[:, NCH:], 0).then_inc(s_zs, 1)
            nc.gpsimd.iota(iota_lt[:, :, :], [[1, J * T], [0, G]], base=0, channel_multiplier=0, **loose)
            nc.gpsimd.iota(nid[:, :], [[1, J]], base=EP, channel_multiplier=J, **loose)
            nc.gpsimd.iota(typc[:, :], [[0, 1]], base=T - D, channel_multiplier=1, **loose)
            for n in range(ST):
                nc.gpsimd.memset(crow[n][:, :], 0.0)
            nc.gpsimd.memset(ones[:, :], 1.0)
            nc.gpsimd.memset(ident[:, :], 0.0)
            nc.gpsimd.memset(lower[:, :], 0.0).then_inc(s_const, 1)
            pool.wait_ge(s_const, 1)
            nc.gpsimd.affine_select(out=ident[:, :], in_=ident[:, :], compare_op=ALU.not_equal, fill=1.0,
                                    base=0, pattern=[[-1, P]], channel_multiplier=1)
            nc.gpsimd.affine_select(out=lower[:, :], in_=lower[:, :], compare_op=ALU.is_ge, fill=1.0,
                                    base=0, pattern=[[-1, P]], channel_multiplier=1).then_inc(s_const, 1)

            passed = [0]

            def follow(ins):
                passed[0] += 1
                ins.then_inc(s_cen, 1)
                pool.wait_ge(s_cen, passed[0])

            def sums(rows, result):
                w = D // 2
                while w:
                    to = ws[:, :, 0:w] if w > 1 else result.unsqueeze(2)
                    follow(nc.gpsimd.tensor_tensor(to, rows[:, :, 0:w], rows[:, :, w:2 * w], ALU.add))
                    rows, w = ws, w // 2

            pool.wait_ge(s_x, 16)
            sums(xs, st[2][:, :])
            follow(nc.gpsimd.tensor_scalar(st[2][:, :], st[2][:, :], 1.0 / D, None, ALU.mult))
            follow(nc.gpsimd.tensor_tensor(hs[:, :, :], xs[:, :, :], st[2][:, :].unsqueeze(2).to_broadcast([P, J, D]),
                                           ALU.subtract))
            follow(nc.gpsimd.tensor_tensor(ws[:, :, :], hs[:, :, :], hs[:, :, :], ALU.mult))
            sums(ws, st[0][:, :])
            nc.gpsimd.tensor_scalar(st[0][:, :], st[0][:, :], 1.0 / D, EPS, ALU.mult, ALU.add).then_inc(s_sq, 1)

            def edge_pass(q):
                table = tab if q < 3 else ytab
                if q < 3:
                    pool.wait_ge(s_tab, 16 * (1 + q * NG))
                else:
                    for y in range(2):
                        pool.wait_ge(s_yd[y], 16 * NG * (q - 2))

                def step(s, i, k, live):
                    pool.wait_ge(s_idx, q * IDXF + s + 1)
                    since(pool, s_turn, q * NS + s - (K - 1))
                    pool.sem_inc(s_go_pool, 1)
                    for g in range(G):
                        if any(is_at(s, unit) for unit in PADDED) and g % ST == ST - 1:
                            continue
                        nc.gpsimd.indirect_dma_start(gat[:, k, g // ST, g % ST, :], None, table[:, :],
                                                     bass.IndirectOffsetOnAxis(ap=idx[:, k, g:g + 1], axis=0)
                                                     ).then_inc(s_gat[k], 16)
                steps(pool, NI, K, step, tail=1)
                for k in range(K):
                    pool.wait_ge(s_dump[k], 16 * NI * (q + 1))
                if q == 0:
                    pool.wait_ge(s_endi, 1)
                for j in range(J):
                    nc.gpsimd.indirect_dma_start(es[:, j, :], None, scans[:, :],
                                                 bass.IndirectOffsetOnAxis(ap=end_i[:, j:j + 1], axis=0)
                                                 ).then_inc(s_ends[j // JG], 16)
            edge_pass(0)
            pool.wait_ge(s_zero, 16 * zero_parts)
            for j in range(J):
                if j % JG == 0:
                    pool.wait_ge(s_sprd, j // JG + 1)
                nc.gpsimd.indirect_dma_start(spread[:, :], bass.IndirectOffsetOnAxis(ap=start_i[:, j:j + 1], axis=0),
                                             ax[:, j, :], None).then_inc(s_scat, 16)
            for q in range(1, NPASS):
                edge_pass(q)

        @block.scalar
        def _(act):
            act.wait_ge(s_zs, 1)
            act.wait_ge(s_edge, 16)
            act.wait_ge(s_x, 16)
            for z in range(zero_parts):
                r = min(zero_per, zero_rows - z * zero_per)
                act.dma_start(spread[z * zero_per:z * zero_per + r, :].rearrange("(p r) d -> p (r d)", p=P),
                              zero[:, 0:r // P * AW]).then_inc(s_zero, 16)

            roots = [0]

            def root(c=slice(0, J)):
                roots[0] += 1
                act.wait_ge(s_sq, roots[0])
                nc.scalar.activation(st[1][:, c], st[0][:, c], ACT.Sqrt).then_inc(s_rt, 1)

            def keep_transposed(name, g):
                c = ORDER_T.index((name, g))
                act.wait_ge(s_lt, c + 1)
                since(act, s_lm, features_used(c))
                nc.scalar.copy(tsl[:, c % 2, :], wide(c % 2)).then_inc(s_lc, 1)

            def typed(m, g, some=range(JG)):
                for j in range(g * JG + some[0], g * JG + some[-1] + 1):
                    act.wait_ge(s_ym, m * J + j + 1)
                    y = j // 5
                    since(act, s_yd[y % 2], 16 * (m * NG + y // 2))
                    nc.scalar.copy(ysl[:, y % 2, j % 5, :], bank(4 + j % 2)).then_inc(s_ya, 1)

            def group(g):
                return slice(g * JG, g * JG + JG)

            def edge_pass(q):
                lag = 3 if q == MLP else 1

                def step(s, i, k, live):
                    b = k % 2
                    if q == MLP and live(0):
                        act.wait_ge(s_axe[k // 2], 32 * (i + 1))
                        since(act, s_turn, q * NS + s - 1)
                        for to, first in ((axf, 0), (axl, T)):
                            last = nc.scalar.copy(to[:, b, :, :, :].rearrange("p g t d -> p t g d"),
                                                  axe[:, k, :, :, first:first + D])
                        last.then_inc(s_axc, 1)
                    if q == MLP and live(1):
                        act.wait_ge(s_hsum, s)
                        nc.scalar.activation(hsm[:, 1 - b, :], hsm[:, 1 - b, :], ACT.Relu).then_inc(s_relu, 1)
                    if q == MLP and live(2):
                        act.wait_ge(s_mlp, s - 1)
                        since(act, s_scan, q * NS + s - 3)
                        nc.scalar.activation(zed[:, b, :], bank(6, SH), ACT.Relu,
                                             bias=eb2[:, 0:1]).then_inc(s_zed, 1)
                        act.wait_ge(s_wsum, s - 1)
                        nc.scalar.copy(inv_s[:, bass.ds((s - 2) * G, G)], bank(7, G)).then_inc(s_wev, 1)
                    if live(lag):
                        i1, k1 = lagged(i, k, lag)
                        act.wait_ge(s_back, q * NS + s - lag + 1)
                        since(act, s_dump[k1], 16 * (q * NI + i1))
                        nc.scalar.copy(dmp[:, k1, :, :, :],
                                       bank(2 + k1 % 2, G * D).rearrange("p (g t d) -> p t g d", g=GH, t=ST)
                                       ).then_inc(s_evac, 1)
                steps(act, NI, K, step, lag)

            root()
            root()
            act.wait_ge(s_w, 16 * n_w)
            edge_pass(0)
            root()
            for t in range(NG + 2):
                if t < NG:
                    keep_transposed("g1", t)
                if 0 <= t - 1 < NG:
                    keep_transposed("g2", t - 1)
                if 0 <= t - 2 < NG:
                    keep_transposed("ab", t - 2)
                if t < NG:
                    act.wait_ge(s_le, PLAIN.index(("g1", t)) + 1)
                    nc.scalar.activation(hs[:, group(t), :], hs[:, group(t), :], ACT.Gelu).then_inc(s_go, 1)
                if 0 <= t - 1 < NG:
                    root(group(t - 1))
            edge_pass(1)
            for g in range(NG):
                root(group(g))
            for g in range(NG):
                keep_transposed("sf", g)
            edge_pass(2)
            for t in range(NG + 1):
                if t > 0:
                    keep_transposed("y0", t - 1)
                if t < NG:
                    keep_transposed("ng", t)
                if t > 0:
                    typed(0, t - 1, range(JG // 2))
                if t < NG:
                    root(group(t))
                if t > 0:
                    typed(0, t - 1, range(JG // 2, JG))
            for g in range(NG):
                keep_transposed("r1", g)
            edge_pass(3)
            for g in range(NG):
                keep_transposed("y1", g)
                typed(1, g)
            for g in range(NG):
                keep_transposed("r2", g)
            edge_pass(4)
            act.wait_ge(s_zero, 16 * zero_parts)

        @block.vector
        def _(dve):
            v = nc.vector
            chained, roots = [0], [0]

            def link(ins):
                chained[0] += 1
                ins.then_inc(s_v, 1)
                dve.wait_ge(s_v, chained[0])

            def root_input(made):
                made.then_inc(s_sq, 1)

            def rsqrt(result, c=slice(0, J)):
                roots[0] += 1
                dve.wait_ge(s_rt, roots[0])
                link(v.reciprocal(result, st[1][:, c]))

            def cols(a, w=J):
                return a.unsqueeze(2).to_broadcast([P, w, D])

            def rows(a, n=J):
                return a[:, :].unsqueeze(1).to_broadcast([P, n, D])

            def group(g):
                return slice(g * JG, g * JG + JG)

            def centre(c):
                link(v.tensor_reduce(out=st[0][:, c], in_=xs[:, c, :], axis=AX.X, op=ALU.add))
                link(v.tensor_scalar(st[2][:, c], st[0][:, c], 1.0 / D, None, ALU.mult))
                link(v.tensor_tensor(hs[:, c, :], xs[:, c, :], cols(st[2][:, c], JG), ALU.subtract))
                link(v.tensor_tensor(ws[:, c, :], hs[:, c, :], hs[:, c, :], ALU.mult))
                link(v.tensor_reduce(out=st[0][:, c], in_=ws[:, c, :], axis=AX.X, op=ALU.add))
                root_input(v.tensor_scalar(st[0][:, c], st[0][:, c], 1.0 / D, EPS, ALU.mult, ALU.add))

            def norm(c):
                rsqrt(st[2][:, c], c)
                return v.scalar_tensor_tensor(out=hs[:, c, :], in0=hs[:, c, :], scalar=0.0,
                                              in1=cols(st[2][:, c], JG), op0=ALU.max, op1=ALU.mult)

            def product(name, g, write):
                key = (name, g)
                dve.wait_ge(s_lm, ORDER_M.index(key) + 1)
                write(group(g), wide(product_slot(key)).rearrange("p (j d) -> p j d", d=D)).then_inc(s_le, 1)

            def products(name, write):
                for g in range(NG):
                    product(name, g, write)
                dve.wait_ge(s_le, plain_until(name))

            def end_rows(q, g):
                c = group(g)
                dve.wait_ge(s_mid, 16 * (q + 1))
                link(v.tensor_tensor(share[:, :, :], rows(mid, JG), cols(cross[:, c], JG), ALU.mult))
                dve.wait_ge(s_ends[g], 16 * JG * (q + 1))
                link(v.tensor_tensor(es[:, c, :], es[:, c, :], share[:, :, :], ALU.max if q == MLP else ALU.add))

            def split(f, q, r):
                link(v.tensor_scalar(q, f, 1.0 / J, -(J - 1) / (2.0 * J), ALU.mult, ALU.add))
                link(v.tensor_scalar(q, q, ROUND, None, ALU.add))
                link(v.tensor_scalar(q, q, ROUND, None, ALU.subtract))
                link(v.scalar_tensor_tensor(out=r, in0=q, scalar=-float(J), in1=f, op0=ALU.mult, op1=ALU.add))

            dve.wait_ge(s_edge, 16)
            link(v.tensor_copy(fa, src_i[:, 0:NCH]))
            split(fa, fb, lo_s[:, :])
            link(v.tensor_copy(hi_s[:, :], fb))
            dve.wait_ge(s_iota, 1)

            def count_sources(s, i, k, live):
                b = k % 2
                since(dve, s_hist, s - 1)
                for rows_, ids, vals, w in ((oh[:, b, :, :], iota_hi, hi_s, P), (ol[:, b, :, :], iota_lo, lo_s, J)):
                    last = v.tensor_tensor(rows_, ids[:, :, :],
                                           vals[:, bass.ds(s * HB, HB)].unsqueeze(1).to_broadcast([P, w, HB]),
                                           ALU.is_equal)
                last.then_inc(s_oh, 1)
                if is_at(s, PEEL * 2 - 1):
                    dve.wait_ge(s_row, 80)
                    v.tensor_tensor(keep_r, row_d.bitcast(i32), row_p.bitcast(i32), ALU.is_equal)
                    v.tensor_copy(typ_r, row_t.bitcast(i32)).then_inc(s_flag, 1)
            steps(dve, NHB // 2, 2, count_sources)

            rsqrt(st[2][:, :])
            dve.wait_ge(s_hist, NHB)
            root_input(v.tensor_scalar(st[0][:, :], bank(0, J), 1.0, None, ALU.max))
            rsqrt(odeg[:, :])
            link(v.tensor_tensor(odeg[:, :], odeg[:, :], st[2][:, :], ALU.mult))
            v.scalar_tensor_tensor(out=ws[:, :, :], in0=hs[:, :, :], scalar=0.0, in1=cols(odeg[:, :]),
                                   op0=ALU.max, op1=ALU.mult).then_inc(s_tabrdy, 1)

            def fill_index(q):
                v.tensor_copy(idx[:, :, :].rearrange("p k g -> p (k g)"), idx_tab[q][:, 0:K * G]).then_inc(s_idx, K)
            fill_index(0)

            dve.wait_ge(s_row, 80)
            v.scalar_tensor_tensor(out=srct_i[:, 0:NCH], in0=fa, scalar=float(T), in1=typ_e.bitcast(i32),
                                   op0=ALU.mult, op1=ALU.add)
            dve.wait_ge(s_const, 2)
            link(v.tensor_scalar(typc[D:P, :], typc[D:P, :], -float(D), None, ALU.add))
            link(v.memset(pair[:, :], 0.0))
            for n in range(ST):
                link(v.memset(pair[D * n:D * n + D, n:n + 1], 1.0))

            link(v.tensor_copy(fa, dst_e.bitcast(i32)))
            split(fa, fb, fa)
            v.tensor_copy(hi_s[:, :], fb)
            link(v.scalar_tensor_tensor(out=lo_s[:, :], in0=fa, scalar=float(T), in1=typ_e.bitcast(i32),
                                        op0=ALU.mult, op1=ALU.add))

            dve.wait_ge(s_w, 16 * n_w)
            dve.wait_ge(s_rowd, 32)
            link(v.tensor_tensor(bd["ea"][:, :], bd["ea"][:, :], bd["eb"][:, :], ALU.subtract))
            for n in range(2):
                for b in range(NB):
                    last = v.tensor_tensor(wprod[:, :, b, :], bas[n][:, b, :].unsqueeze(1).to_broadcast([P, T, D]),
                                           com[n][:, :, b:b + 1].to_broadcast([P, T, D]), ALU.mult)
                link(last)
                for h in range(2):
                    half = slice(D * h, D * h + D)
                    last = v.tensor_reduce(out=wz[n][half, h, :].rearrange("p (t o) -> p t o", t=T),
                                           in_=wprod[half, :, :, :].rearrange("p t b o -> p t o b"),
                                           axis=AX.X, op=ALU.add)
                link(last)

            def edge_pass(q):
                scale = wgt_tab[q]
                link(v.memset(scn[:, 1, SH - 1:SH], 0.0))
                if q == MLP:
                    dve.wait_ge(s_crs, 1)
                    v.tensor_copy(fil[:, 1, SH - 1:SH], bank(6, 1))
                    link(v.tensor_copy(fit[:, 1, SH - 1:SH], ps[:, 512 * 6 + 1:512 * 6 + 2]))

                def step(s, i, k, live):
                    b = k % 2
                    if live(0):
                        dve.wait_ge(s_gat[k], gathered(q, s, i, k))
                        v.tensor_copy(idx[:, k, :], idx_tab[q][:, bass.ds((s + K) * G, G)]).then_inc(s_idx, 1)
                        if scale is not None:
                            rows4 = gat[:, k, :, :, :].rearrange("p g t d -> p (g t) d")
                            v.tensor_tensor(rows4, rows4,
                                            scale[:, bass.ds(s * G, G)].unsqueeze(2).to_broadcast([P, G, D]),
                                            ALU.mult).then_inc(s_scl, 1)
                    if q == 0 and live(0):
                        since(dve, s_cc, s - 1)
                        v.tensor_tensor(oh[:, b, :, 0:G], iota_hi[:, :, 0:G],
                                        hi_s[:, bass.ds(s * G, G)].unsqueeze(1).to_broadcast([P, P, G]),
                                        ALU.is_equal)
                        v.tensor_tensor(olt[:, b, :, :], iota_lt[:, :, :],
                                        lo_s[:, bass.ds(s * G, G)].unsqueeze(1).to_broadcast([P, J * T, G]),
                                        ALU.is_equal).then_inc(s_coh, 1)
                    if q == MLP and live(0):
                        dve.wait_ge(s_turn, q * NS + s + 1)
                        dve.wait_ge(s_keep[k // 2], 32 * (q * NI + i + 1))
                        since(dve, s_fil, s)
                        v.tensor_tensor_scan(fil[:, b, :], keep[:, k, :], bank(4 + b, SH),
                                             fil[:, 1 - b, SH - 1:SH], ALU.mult, ALU.add)
                        v.tensor_tensor_scan(fit[:, b, :], keep[:, k, :], bank(4 + b)[:, SH:2 * SH],
                                             fit[:, 1 - b, SH - 1:SH], ALU.mult, ALU.add).then_inc(s_fil, 1)
                        dve.wait_ge(s_fil, s + 1)
                        since(dve, s_mlp, s - 1)
                        v.tensor_tensor(hsm[:, b, :], bank(b, SH), fil[:, b, :], ALU.add).then_inc(s_hsum, 1)
                        since(dve, s_wsum, s - 1)
                        v.scalar_tensor_tensor(out=tpr[:, b, :], in0=typb[:, k, :], scalar=typc[:, 0:1],
                                               in1=fit[:, b, :], op0=ALU.is_equal, op1=ALU.mult
                                               ).then_inc(s_tpr, 1)
                    if live(1):
                        i1, k1 = lagged(i, k, 1)
                        if q == MLP:
                            dve.wait_ge(s_zed, s)
                            values, op = zed[:, 1 - b, :], ALU.max
                        else:
                            dve.wait_ge(s_turn, q * NS + s)
                            dve.wait_ge(s_keep[k1 // 2], 32 * (q * NI + i1 + 1))
                            values, op = bank(1 - b, SH), ALU.add
                        since(dve, s_scan, q * NS + s - 1)
                        since(dve, s_back, q * NS + s - 2)
                        v.tensor_tensor_scan(scn[:, 1 - b, :], keep[:, k1, :], values,
                                             scn[:, b, SH - 1:SH], ALU.mult, op).then_inc(s_scan, 1)
                steps(dve, NI, K, step, 1, tail=1)

            edge_pass(0)
            dve.wait_ge(s_cc, NS)
            link(v.tensor_copy(cnt[:, :, :].rearrange("p j t -> p (j t)"), bank(4, J * T)))
            link(v.tensor_reduce(out=deg[:, :], in_=cnt[:, :, :], axis=AX.X, op=ALU.add))
            v.tensor_tensor_scan(csum[:, :], ones[:, :], deg[:, :], 0.0, ALU.mult, ALU.add).then_inc(s_tot, 1)
            link(v.tensor_scalar(dmask[:, :], deg[:, :], 1.0, None, ALU.min))
            dve.wait_ge(s_pre, 1)
            link(v.tensor_copy(pre[:, :], bank(6, 1)))
            link(v.tensor_scalar(csum[:, :], csum[:, :], pre[:, 0:1], None, ALU.add))
            v.tensor_scalar(end_i[:, :], csum[:, :], -1.0, 0.0, ALU.add, ALU.max).then_inc(s_endi, 1)
            link(v.tensor_tensor(st[2][:, :], csum[:, :], deg[:, :], ALU.subtract))
            link(v.tensor_tensor(st[2][:, :], st[2][:, :], nid[:, :], ALU.subtract))
            link(v.tensor_tensor(st[2][:, :], st[2][:, :], dmask[:, :], ALU.mult))
            link(v.tensor_tensor(start_i[:, :], st[2][:, :], nid[:, :], ALU.add))
            link(v.tensor_tensor(cross[:, :], csum[:, :], deg[:, :], ALU.subtract))
            link(v.tensor_scalar(cross[:, :], cross[:, :], float(EH), None, ALU.is_lt))
            link(v.scalar_tensor_tensor(out=cross[:, :], in0=csum[:, :], scalar=float(EH), in1=cross[:, :],
                                        op0=ALU.is_gt, op1=ALU.mult))
            root_input(v.tensor_scalar(st[0][:, :], deg[:, :], 1.0, None, ALU.max))
            rsqrt(gcnf[:, :])
            link(v.tensor_tensor(gcnf[:, :], gcnf[:, :], dmask[:, :], ALU.mult))
            link(v.reciprocal(meanf[:, :], st[0][:, :]))
            link(v.tensor_tensor(meanf[:, :], meanf[:, :], dmask[:, :], ALU.mult))
            link(v.tensor_scalar(cnt[:, :, :], cnt[:, :, :], 1.0, None, ALU.max))
            link(v.reciprocal(ax[:, :, D:AW], cnt[:, :, :]))
            link(v.tensor_tensor(xs[:, :, :], xs[:, :, :], rows(bias["g2"]), ALU.add))
            for t in range(NG + 2):
                if t < NG:
                    c = group(t)
                    end_rows(0, t)
                    v.tensor_tensor(ws[:, c, :], es[:, c, :], cols(gcnf[:, c], JG), ALU.mult).then_inc(s_lin, 1)
                if 0 <= t - 2 < NG:
                    norm(group(t - 2)).then_inc(s_lin, 1)
                if t < NG:
                    product("g1", t, lambda c, o: v.tensor_tensor(hs[:, c, :], o, rows(bias["g1"], JG), ALU.add))
                if 0 <= t - 1 < NG:
                    c = group(t - 1)
                    product("g2", t - 1, lambda c, o: v.tensor_tensor(xs[:, c, :], o, xs[:, c, :], ALU.add))
                    dve.wait_ge(s_le, PLAIN.index(("g2", t - 1)) + 1)
                    centre(c)
                if 0 <= t - 2 < NG:
                    product("ea", t - 2, lambda c, o: v.tensor_tensor(ax[:, c, 0:D], o, rows(bias["ea"], JG), ALU.add))
                    product("eb", t - 2, lambda c, o: v.tensor_copy(ws[:, c, :], o))
                    dve.wait_ge(s_le, PLAIN.index(("eb", t - 2)) + 1)
                    dve.sem_inc(s_sprd, 1)
                    dve.sem_inc(s_tabrdy, 1)

            link(v.tensor_tensor(es[:, :, :], ax[:, :, 0:D], cols(cross[:, :]), ALU.mult))
            link(v.tensor_tensor(cnt[:, :, :], ax[:, :, D:AW], cross[:, :].unsqueeze(2).to_broadcast([P, J, T]), ALU.mult))
            link(v.tensor_reduce(out=crow[0][:, D:P], in_=es[:, :, :].rearrange("p j d -> p d j"), axis=AX.X, op=ALU.add))
            v.tensor_copy(crow[1][:, D:P - T], crow[0][:, D + T:P])
            v.tensor_reduce(out=crow[1][:, P - T:P], in_=cnt[:, :, :].rearrange("p j t -> p t j"), axis=AX.X,
                            op=ALU.add).then_inc(s_cross, 1)
            fill_index(1)
            edge_pass(1)
            for t in range(NG + 1):
                if t > 0:
                    norm(group(t - 1)).then_inc(s_tabrdy, 1)
                if t < NG:
                    c = group(t)
                    end_rows(1, t)
                    link(v.tensor_tensor(es[:, c, :], es[:, c, :], cols(dmask[:, c], JG), ALU.mult))
                    link(v.tensor_tensor(xs[:, c, :], xs[:, c, :], es[:, c, :], ALU.add))
                    centre(c)

            fill_index(2)
            dve.wait_ge(s_tabrdy, 1 + 2 * NG)
            dve.sem_inc(s_lin, NG)
            products("sf", lambda c, o: v.tensor_tensor(rs[:, c, :], o, rows(bias["sf"], JG), ALU.add))
            link(v.tensor_tensor(xs[:, :, :], xs[:, :, :], rs[:, :, :], ALU.add))
            link(v.tensor_tensor(xs[:, :, :], xs[:, :, :], rows(bias["ng"]), ALU.add))
            edge_pass(2)

            for t in range(NG + 1):
                if t > 0:
                    norm(group(t - 1)).then_inc(s_lin, 1)
                if t < NG:
                    c = group(t)
                    end_rows(2, t)
                    v.tensor_tensor(ws[:, c, :], es[:, c, :], cols(meanf[:, c], JG), ALU.mult).then_inc(s_lin, 1)
                    product("ng", t, lambda c, o: v.tensor_tensor(xs[:, c, :], o, xs[:, c, :], ALU.add))
                    dve.wait_ge(s_le, PLAIN.index(("ng", t)) + 1)
                    centre(c)
            fill_index(3)
            dve.wait_ge(s_lin, BY_VECTOR.index(("r1", 0)))
            dve.sem_inc(s_lin, NG)
            products("r1", lambda c, o: v.tensor_tensor(rs[:, c, :], o, rows(bias["r1"], JG), ALU.add))
            edge_pass(3)

            for t in range(NG):
                c = group(t)
                end_rows(3, t)
                link(v.tensor_tensor(es[:, c, :], es[:, c, :], cols(dmask[:, c], JG), ALU.mult))
                link(v.tensor_tensor(es[:, c, :], es[:, c, :], rs[:, c, :], ALU.add))
                v.tensor_scalar(hs[:, c, :], es[:, c, :], 0.0, None, ALU.max).then_inc(s_lin, 1)
            fill_index(4)
            dve.wait_ge(s_lin, BY_VECTOR.index(("r2", 0)))
            dve.sem_inc(s_lin, NG)
            products("r2", lambda c, o: v.tensor_tensor(rs[:, c, :], o, rows(bias["r2"], JG), ALU.add))
            link(v.tensor_tensor(xs[:, :, :], xs[:, :, :], rs[:, :, :], ALU.add))
            edge_pass(4)
            for t in range(NG):
                c = group(t)
                end_rows(4, t)
                link(v.tensor_tensor(es[:, c, :], es[:, c, :], cols(dmask[:, c], JG), ALU.mult))
                v.tensor_tensor(ws[:, c, :], es[:, c, :], xs[:, c, :], ALU.add).then_inc(s_fin, 1)

        @block.tensor
        def _(pe):
            pe.wait_ge(s_const, 2)

            def count_sources(s, i, k, live):
                b = k % 2
                pe.wait_ge(s_oh, s + 1)
                for c in range(HB):
                    last = nc.tensor.matmul(bank(0, J), oh[:, b, :, c], ol[:, b, :, c],
                                            start=is_at(s, 0) and c == 0,
                                            stop=is_at(s, NHB - 1) and c == HB - 1)
                last.then_inc(s_hist, 1)
            steps(pe, NHB // 2, 2, count_sources, tail=1)

            def turn(name, g, rows):
                key = (name, g)
                c = ORDER_T.index(key)
                if name == "g2":
                    pe.wait_ge(s_go, g + 1)
                else:
                    pe.wait_ge(s_lin, BY_VECTOR.index(key) + 1)
                since(pe, s_lc, c - 1)
                for q in range(JG // 2):
                    last = nc.tensor.transpose(wide(c % 2)[:, q * P:q * P + P],
                                               rows[:, g * JG + 2 * q:g * JG + 2 * q + 2, :].rearrange("p j d -> p (j d)"),
                                               ident[:, :])
                last.then_inc(s_lt, 1)

            def multiply(name, g, features=None):
                key = (name, g)
                c = ORDER_T.index((features or name, g))
                pe.wait_ge(s_lc, c + 1)
                since(pe, s_le, slot_read(key))
                for q in range(JG // 2):
                    last = nc.tensor.matmul(wide(product_slot(key))[:, q * P:q * P + P],
                                            tsl[:, c % 2, q * P:q * P + P], bd[name][:, :], start=True, stop=True)
                last.then_inc(s_lm, 1)

            def products(name, rows):
                turn(name, 0, rows)
                for g in range(NG):
                    if g + 1 < NG:
                        turn(name, g + 1, rows)
                    multiply(name, g)

            def typed(m, g):
                c = ORDER_T.index((f"y{m}", g))
                pe.wait_ge(s_lc, c + 1)
                for j in range(g * JG, g * JG + JG):
                    since(pe, s_ya, m * J + j - 1)
                    q = (j - g * JG) // 2
                    last = nc.tensor.matmul(bank(4 + j % 2), tsl[:, c % 2, q * P:q * P + P],
                                            wz[m][:, j % 2, :], start=True, stop=True)
                    last.then_inc(s_ym, 1)
                pe.wait_ge(s_ym, m * J + g * JG + JG)
                pe.sem_inc(s_lm, 1)

            def edge_pass(q):
                mlp = q == MLP
                lag = 2 if mlp else 1
                scaled = sum(w is not None for w in wgt_tab[:q])

                def by_edge(a, g):
                    return a.rearrange("d (p g) -> d g p", g=GH)[:, g, :]

                def step(s, i, k, live):
                    b = k % 2
                    if live(0):
                        if wgt_tab[q] is not None:
                            pe.wait_ge(s_scl, scaled * NS + s + 1)
                        else:
                            pe.wait_ge(s_gat[k], gathered(q, s, i, k))
                        if mlp:
                            since(pe, s_hsum, s - 1)
                        else:
                            since(pe, s_scan, q * NS + s - 1)
                        pe.sem_inc(s_go_pe, 1)
                        for g in range(GH):
                            last = nc.tensor.transpose(by_edge(bank(b, SH), g),
                                                       gat[:, k, g, :, :].rearrange("p t d -> p (t d)"), ident[:, :])
                        if mlp:
                            pe.wait_ge(s_axc, s + 1)
                            since(pe, s_tpr, s - 1)
                            pe.sem_inc(s_go_pe, 1)
                            for to, rows in ((bank(4 + b, SH), axf), (bank(4 + b)[:, SH:2 * SH], axl)):
                                for g in range(GH):
                                    last = nc.tensor.transpose(by_edge(to, g), rows[:, b, g, :, :].rearrange("p t d -> p (t d)"),
                                                               ident[:, :])
                        last.then_inc(s_turn, 1)
                    if q == 0 and live(0):
                        pe.wait_ge(s_coh, s + 1)
                        for g in range(G):
                            last = nc.tensor.matmul(bank(4, J * T), oh[:, b, :, g], olt[:, b, :, g],
                                                    start=is_at(s, 0) and g == 0,
                                                    stop=is_at(s, NS - 1) and g == G - 1)
                        last.then_inc(s_cc, 1)
                    if mlp and live(1):
                        pe.wait_ge(s_relu, s)
                        since(pe, s_zed, s - 1)
                        pe.sem_inc(s_go_pe, 1)
                        nc.tensor.matmul(bank(6, SH), bd["w2"][:, :], hsm[:, 1 - b, :],
                                         start=True, stop=True).then_inc(s_mlp, 1)
                        pe.wait_ge(s_tpr, s)
                        since(pe, s_wev, s - 1)
                        for g in range(GH):
                            last = nc.tensor.matmul(bank(7)[:, ST * g:ST * g + ST], by_edge(tpr[:, 1 - b, :], g),
                                                    pair[:, :], start=True, stop=True)
                        last.then_inc(s_wsum, 1)
                    if live(lag):
                        b1 = (k - lag) % 2
                        pe.wait_ge(s_scan, q * NS + s - lag + 1)
                        since(pe, s_evac, q * NS + s - lag - 1)
                        pe.sem_inc(s_go_pe, 1)
                        for g in range(GH):
                            last = nc.tensor.transpose(bank(2 + b1)[:, g * P:g * P + P],
                                                       by_edge(scn[:, b1, :], g), ident[:, :])
                        last.then_inc(s_back, 1)
                steps(pe, NI, K, step, lag, tail=1)

            edge_pass(0)
            pe.wait_ge(s_tot, 1)
            nc.tensor.matmul(bank(6, 1), lower[:, :], csum[:, J - 1:J], start=True, stop=True).then_inc(s_pre, 1)
            for t in range(NG + 2):
                if t < NG:
                    turn("g1", t, ws)
                if 0 <= t - 1 < NG:
                    turn("g2", t - 1, hs)
                if t < NG:
                    multiply("g1", t)
                if 0 <= t - 2 < NG:
                    turn("ab", t - 2, hs)
                if 0 <= t - 1 < NG:
                    multiply("g2", t - 1)
                if 0 <= t - 2 < NG:
                    multiply("ea", t - 2, "ab")
                    multiply("eb", t - 2, "ab")
            pe.wait_ge(s_le, plain_until("eb"))
            pe.wait_ge(s_cross, 1)
            for n in range(2):
                last = nc.tensor.matmul(ps[:, 512 * 6 + n:512 * 6 + n + 1], crow[n][:, :], ones[:, 0:1],
                                        start=True, stop=True)
            last.then_inc(s_crs, 1)
            edge_pass(1)
            products("sf", hs)
            pe.wait_ge(s_le, plain_until("sf"))
            edge_pass(2)
            for t in range(NG + 1):
                if t > 0:
                    turn("y0", t - 1, hs)
                if t < NG:
                    turn("ng", t, ws)
                    multiply("ng", t)
                if t > 0:
                    typed(0, t - 1)
            products("r1", hs)
            pe.wait_ge(s_le, plain_until("r1"))
            pe.wait_ge(s_ya, J)
            edge_pass(3)
            for g in range(NG):
                turn("y1", g, hs)
                typed(1, g)
            products("r2", hs)
            pe.wait_ge(s_le, plain_until("r2"))
            pe.wait_ge(s_ya, 2 * J)
            edge_pass(4)


def kernel(**inputs):
    import numpy as _np
    import concourse.bacc as _bacc
    from concourse import mybir as _mybir
    from concourse.bass_utils import run_bass_kernel_spmd as _run

    a = {k: _np.asarray(v) for k, v in inputs.items()}

    def pad(row, value):
        return _np.concatenate([row, _np.full(EP - E, value, row.dtype)])

    def by_superchunk(row):
        return _np.ascontiguousarray(row.reshape(ST, NS, P, GH).transpose(2, 1, 3, 0).reshape(P, NCH))

    dst = pad(a["dst"], NPAD - 1)
    src = pad(a["src"], NPAD - 1)
    typ = pad(a["edge_type_8"], 0)
    before = _np.concatenate([_np.full(1, -1, dst.dtype), dst[:-1]])
    x = _np.concatenate([a["x"], _np.zeros((NPAD - N, D), a["x"].dtype)])
    data = [
        ("x", x), ("src", by_superchunk(src)), ("dst", by_superchunk(dst)), ("typ", by_superchunk(typ)),
        ("wgt", by_superchunk(pad(a["edge_weight"], 0))),
        ("dst_row", dst.reshape(P, NCH)), ("prev_row", before.reshape(P, NCH)), ("typ_row", typ.reshape(P, NCH)),
        ("gcn_w1", a["L0_gnn_w1"]), ("gcn_b1", a["L0_gnn_b1"]), ("gcn_w2", a["L0_gnn_w2"]), ("gcn_b2", a["L0_gnn_b2"]),
        ("edge_w1", a["L1_gnn_W1"]), ("edge_b1", a["L1_gnn_b1"]), ("edge_w2", a["L1_gnn_W2"]), ("edge_b2", a["L1_gnn_b2"]),
        ("self_wT", a["L2_gnn_W_self"].T), ("self_b", a["L2_gnn_b_self"]),
        ("neigh_wT", a["L2_gnn_W_neigh"].T), ("neigh_b", a["L2_gnn_b_neigh"]),
        ("basis1", a["L3_gnn_basis1"]), ("comp1", a["L3_gnn_comp1"]), ("root1", a["L3_gnn_root1"]), ("bias1", a["L3_gnn_bias1"]),
        ("basis2", a["L3_gnn_basis2"]), ("comp2", a["L3_gnn_comp2"]), ("root2", a["L3_gnn_root2"]), ("bias2", a["L3_gnn_bias2"]),
    ]
    nc = _bacc.Bacc("TRN2", target_bir_lowering=False, num_devices=1)
    arrays, args = {}, []
    for name, value in data:
        arrays[f"in_{name}"] = _np.ascontiguousarray(value)
        args.append(nc.dram_tensor(f"in_{name}", value.shape, _mybir.dt.from_np(value.dtype), kind="ExternalInput").ap())
    out = nc.dram_tensor("out_0", (N, D), _mybir.dt.float32, kind="ExternalOutput").ap()
    gnn_kernel(nc, *args, out)
    r = _run(nc, [arrays], core_ids=[0])
    return r.results[0]["out_0"]
```
